# Optimizing a Trainium2 kernel written in Bass

```python
import numpy as np
import jax
import jax.numpy as jnp

def _softmax(x, axis=-1):
    return jax.nn.softmax(x, axis=axis)

def _gelu(x):
    return jax.nn.gelu(x, approximate=True)

def _silu(x):
    return jax.nn.silu(x)

def _sigmoid(x):
    return jax.nn.sigmoid(x)

def _layernorm(x, axis=-1, eps=1e-05):
    m = jnp.mean(x, axis=axis, keepdims=True)
    v = jnp.var(x, axis=axis, keepdims=True)
    return (x - m) / jnp.sqrt(v + eps)

def _scatter_add(tgt, idx, src, axis=0):
    return tgt.at[idx].add(src)

def _segment_sum(src, seg, n):
    return jax.ops.segment_sum(src, seg, n)
kernel_name = 'mk_macaron_d1_jaxref_r8_44c463'

def setup_inputs(seed: int=0):
    np.random.seed(seed)
    _w = jnp.asarray

    def _L0_attn_setup():
        import jax, jax.numpy as jnp
        import numpy as np
        DIM = 128
        HEADS = 16
        DIM_HEAD = 64
        NUM_FREQS = 16
        INNER = HEADS * DIM_HEAD

        def rotate_half(x):
            x1 = x[..., ::2]
            x2 = x[..., 1::2]
            return jnp.concatenate((-x2, x1), axis=-1)

        def rope_fourier_cache(seq_len, head_dim, num_freqs):
            freqs = 10000.0 ** (-jnp.arange(0, head_dim, 2, dtype=jnp.float32) / head_dim)
            pos = jnp.arange(seq_len, dtype=jnp.float32)[:, None]
            angles = pos * freqs
            sin = jnp.sin(angles)
            cos = jnp.cos(angles)
            sin = jnp.stack([sin, sin], axis=-1).reshape(seq_len, head_dim)
            cos = jnp.stack([cos, cos], axis=-1).reshape(seq_len, head_dim)
            ffreqs = jnp.arange(1, num_freqs + 1, dtype=jnp.float32)
            p = jnp.arange(seq_len, dtype=jnp.float32)[:, None]
            fourier = jnp.concatenate([jnp.sin(p * ffreqs), jnp.cos(p * ffreqs)], axis=-1)
            return (sin, cos, fourier)
        key = jax.random.key(seed)
        ks = jax.random.split(key, 6)
        b, n = (4, 256)
        x = jax.random.normal(ks[0], (b, n, DIM), dtype=jnp.float32)
        w_qkv = jax.random.normal(ks[1], (3 * INNER, DIM), dtype=jnp.float32) * DIM ** (-0.5)
        w_fproj = jax.random.normal(ks[2], (DIM_HEAD, 2 * NUM_FREQS), dtype=jnp.float32) * (2 * NUM_FREQS) ** (-0.5)
        b_fproj = jax.random.normal(ks[3], (DIM_HEAD,), dtype=jnp.float32) * 0.02
        w_out = jax.random.normal(ks[4], (DIM, INNER), dtype=jnp.float32) * INNER ** (-0.5)
        b_out = jax.random.normal(ks[5], (DIM,), dtype=jnp.float32) * 0.02
        return {'x': x, 'w_qkv': w_qkv, 'w_fproj': w_fproj, 'b_fproj': b_fproj, 'w_out': w_out, 'b_out': b_out}
    _L0_attn_in = _L0_attn_setup()

    def _L0_ffn_setup():
        import jax, jax.numpy as jnp
        import numpy as np
        TOPK = 8
        NUM_EXPERTS = 64
        FFN = 384
        CAPACITY = 160

        def _swiglu(x, w1, w2):
            h = x @ w1.T
            x1, x2 = jnp.split(h, 2, axis=-1)
            return x1 * jax.nn.silu(x2) @ w2.T
        key = jax.random.key(seed)
        ks = jax.random.split(key, 6)
        B, S, H = (1, 64, 128)
        scale = 0.02
        return {'hidden_states': jax.random.normal(ks[0], (B, S, H), jnp.float32), 'wg': jax.random.normal(ks[1], (NUM_EXPERTS, H), jnp.float32) * scale, 'shared_w1': jax.random.normal(ks[2], (2 * FFN, H), jnp.float32) * scale, 'shared_w2': jax.random.normal(ks[3], (H, FFN), jnp.float32) * scale, 'expert_w1': jax.random.normal(ks[4], (NUM_EXPERTS, 2 * FFN, H), jnp.float32) * scale, 'expert_w2': jax.random.normal(ks[5], (NUM_EXPERTS, H, FFN), jnp.float32) * scale}
    _L0_ffn_in = _L0_ffn_setup()
    _d = {'L0_attn_x': _L0_attn_in['x'], 'L0_attn_w_qkv': _L0_attn_in['w_qkv'], 'L0_attn_w_fproj': _L0_attn_in['w_fproj'], 'L0_attn_b_fproj': _L0_attn_in['b_fproj'], 'L0_attn_w_out': _L0_attn_in['w_out'], 'L0_attn_b_out': _L0_attn_in['b_out'], 'L0_ffn_wg': _L0_ffn_in['wg'], 'L0_ffn_shared_w1': _L0_ffn_in['shared_w1'], 'L0_ffn_shared_w2': _L0_ffn_in['shared_w2'], 'L0_ffn_expert_w1': _L0_ffn_in['expert_w1'], 'L0_ffn_expert_w2': _L0_ffn_in['expert_w2']}
    _x0 = _d['L0_attn_x']
    _d['L0_attn_x'] = jax.random.normal(jax.random.fold_in(jax.random.key(seed), 1), (8, 256, 128), dtype=_x0.dtype)
    del _x0
    return _d

def reference(L0_attn_x, L0_attn_w_qkv, L0_attn_w_fproj, L0_attn_b_fproj, L0_attn_w_out, L0_attn_b_out, L0_ffn_wg, L0_ffn_shared_w1, L0_ffn_shared_w2, L0_ffn_expert_w1, L0_ffn_expert_w2):

    def _L0_attn_ref(x, w_qkv, w_fproj, b_fproj, w_out, b_out):
        import jax, jax.numpy as jnp
        import numpy as np
        DIM = 128
        HEADS = 16
        DIM_HEAD = 64
        NUM_FREQS = 16
        INNER = HEADS * DIM_HEAD

        def rotate_half(x):
            x1 = x[..., ::2]
            x2 = x[..., 1::2]
            return jnp.concatenate((-x2, x1), axis=-1)

        def rope_fourier_cache(seq_len, head_dim, num_freqs):
            freqs = 10000.0 ** (-jnp.arange(0, head_dim, 2, dtype=jnp.float32) / head_dim)
            pos = jnp.arange(seq_len, dtype=jnp.float32)[:, None]
            angles = pos * freqs
            sin = jnp.sin(angles)
            cos = jnp.cos(angles)
            sin = jnp.stack([sin, sin], axis=-1).reshape(seq_len, head_dim)
            cos = jnp.stack([cos, cos], axis=-1).reshape(seq_len, head_dim)
            ffreqs = jnp.arange(1, num_freqs + 1, dtype=jnp.float32)
            p = jnp.arange(seq_len, dtype=jnp.float32)[:, None]
            fourier = jnp.concatenate([jnp.sin(p * ffreqs), jnp.cos(p * ffreqs)], axis=-1)
            return (sin, cos, fourier)
        b, n, _ = x.shape
        scale = DIM_HEAD ** (-0.5)
        qkv = x @ w_qkv.T
        q, k, v = jnp.split(qkv, 3, axis=-1)

        def to_heads(t):
            return t.reshape(b, n, HEADS, DIM_HEAD).transpose(0, 2, 1, 3)
        q, k, v = (to_heads(q), to_heads(k), to_heads(v))
        sin, cos, fourier = rope_fourier_cache(n, DIM_HEAD, NUM_FREQS)
        fenc = fourier @ w_fproj.T + b_fproj
        fenc = fenc[None, None]
        q = q * cos + rotate_half(q) * sin + fenc
        k = k * cos + rotate_half(k) * sin + fenc
        dots = jnp.einsum('bhid,bhjd->bhij', q, k) * scale
        attn = jax.nn.softmax(dots, axis=-1)
        out = jnp.einsum('bhij,bhjd->bhid', attn, v)
        out = out.transpose(0, 2, 1, 3).reshape(b, n, INNER)
        return out @ w_out.T + b_out

    def _L0_ffn_ref(hidden_states, wg, shared_w1, shared_w2, expert_w1, expert_w2):
        import jax, jax.numpy as jnp
        import numpy as np
        TOPK = 8
        NUM_EXPERTS = 64
        FFN = 384
        CAPACITY = 160

        def _swiglu(x, w1, w2):
            h = x @ w1.T
            x1, x2 = jnp.split(h, 2, axis=-1)
            return x1 * jax.nn.silu(x2) @ w2.T
        B, S, H = hidden_states.shape
        T = B * S
        x = hidden_states.reshape(T, H)
        shared_out = _swiglu(x, shared_w1, shared_w2)
        logits = x.astype(jnp.float32) @ wg.T
        gates = jax.nn.softmax(logits, axis=-1)
        w_topk, idx_topk = jax.lax.top_k(gates, TOPK)
        denom = jnp.maximum(w_topk.sum(-1, keepdims=True), jnp.finfo(jnp.float32).eps)
        w_topk = w_topk / denom
        A = T * TOPK
        flat_e = idx_topk.reshape(A)
        flat_w = w_topk.reshape(A)
        flat_t = jnp.repeat(jnp.arange(T), TOPK)
        order = jnp.argsort(flat_e)
        se, st, sw = (flat_e[order], flat_t[order], flat_w[order])
        counts = jnp.zeros(NUM_EXPERTS, jnp.int32).at[flat_e].add(1)
        starts = jnp.cumsum(counts) - counts
        rank = jnp.arange(A) - starts[se]
        valid = rank < CAPACITY
        buf = jnp.zeros((NUM_EXPERTS, CAPACITY, H), x.dtype).at[se, rank].set(x[st], mode='drop')
        h = jnp.einsum('ech,efh->ecf', buf, expert_w1)
        x1, x2 = jnp.split(h, 2, axis=-1)
        out = jnp.einsum('ecf,ehf->ech', x1 * jax.nn.silu(x2), expert_w2)
        y = out[se, jnp.clip(rank, 0, CAPACITY - 1)]
        y = jnp.where(valid[:, None], y * sw[:, None].astype(y.dtype), 0.0)
        combined = jnp.zeros((T, H), x.dtype).at[st].add(y)
        return (shared_out + combined).reshape(B, S, H)
    x = L0_attn_x
    x = x + 0.5 * _L0_ffn_ref(_layernorm(x, axis=-1), L0_ffn_wg, L0_ffn_shared_w1, L0_ffn_shared_w2, L0_ffn_expert_w1, L0_ffn_expert_w2)
    x = x + _L0_attn_ref(_layernorm(x, axis=-1), L0_attn_w_qkv, L0_attn_w_fproj, L0_attn_b_fproj, L0_attn_w_out, L0_attn_b_out)
    x = x + 0.5 * _L0_ffn_ref(_layernorm(x, axis=-1), L0_ffn_wg, L0_ffn_shared_w1, L0_ffn_shared_w2, L0_ffn_expert_w1, L0_ffn_expert_w2)
    return x

_drawn_inputs = setup_inputs


def setup_inputs(seed=0):
    import zlib

    import numpy as np

    out = dict(_drawn_inputs(seed))
    spreads = {}
    factors = {'L0_attn_b_fproj': 8.0,
     'L0_ffn_wg': 8.0,
     'L0_ffn_shared_w1': 5.809,
     'L0_ffn_shared_w2': 5.805,
     'L0_ffn_expert_w1': 8.0,
     'L0_ffn_expert_w2': 8.0}
    for name, (base, spread) in spreads.items():
        noise = np.random.default_rng([zlib.crc32(name.encode()), seed]).standard_normal(out[name].shape)
        drawn = base * np.exp(spread * noise) if base else spread * noise
        out[name] = jnp.asarray(drawn.astype(out[name].dtype))
    for name, factor in factors.items():
        out[name] = (out[name] * factor).astype(out[name].dtype)
    return out
```

```python
from contextlib import ExitStack

import numpy as np

import concourse.bass as bass
from concourse import mybir

F32 = mybir.dt.float32
BF16 = mybir.dt.bfloat16
I32 = mybir.dt.int32
U32 = mybir.dt.uint32
ALU = mybir.AluOpType
ACT = mybir.ActivationFunctionType
AX = mybir.AxisListType

P = 128
BATCH, SEQ, DIM = 8, 256, 128
TOKENS = BATCH * SEQ
TILES = TOKENS // P
TPB = SEQ // P

HEADS, DH, FREQS = 16, 64, 16
INNER = HEADS * DH
PAIRS = HEADS // 2
SCALE = DH ** -0.5

EXPERTS, TOPK, FFN, CAPACITY = 64, 8, 384, 160
FC = FFN // P
WCOLS = 2 * FFN + FC * DIM
PLACES = EXPERTS * CAPACITY
COLS = PLACES // P
GE = 4
GT = GE * CAPACITY // P
GW = GE * CAPACITY
STEP_GROUPS = 2
STEP_EXPERTS = STEP_GROUPS * GE
STEPS = EXPERTS // STEP_EXPERTS
BLK = 512
BLOCKS = TOKENS // BLK
YROWS = TOKENS * TOPK
FAR = 32768.0
EPS_LN = 1e-5
EPS_F32 = float(np.finfo(np.float32).eps)


def after(eng, sem, count):
    if not isinstance(count, int) or count > 0:
        eng.wait_ge(sem, count)


def ffn(nc, x, consts, w, ydram, xn_dram, ps, tag, out_dram=None):
    wexp, shw, wg = w
    ident, iota_e, iota_p, iota_c, before, ones_bf, tokp1, zeros = consts
    with ExitStack() as ctx:
        def sb(name, shape, dt=F32):
            return ctx.enter_context(nc.sbuf_tensor(f"{tag}_{name}", shape, dt))

        def sem(name):
            return ctx.enter_context(nc.semaphore(f"{tag}_{name}"))

        ring = sb("ring", [P, STEP_EXPERTS, WCOLS])
        take = sb("take", [P, COLS], I32)
        put = sb("put", [P, COLS], I32)
        wk = sb("wk", [P, TILES, TOPK])
        w_landed = [sem(f"w_landed{i}") for i in range(STEP_EXPERTS)]
        half_shared = sb("half_shared", [P, TILES, DIM])
        zeroed = sem("zeroed")
        xn_stored = sem("xn_stored")

        with ExitStack() as rctx:
            def rsb(name, shape, dt=F32):
                return rctx.enter_context(nc.sbuf_tensor(f"{tag}_{name}", shape, dt))

            def rsem(name):
                return rctx.enter_context(nc.semaphore(f"{tag}_{name}"))

            xn = rsb("xn", [P, TILES, DIM])
            xnT = rsb("xnT", [P, TOKENS])
            sq = half_shared
            st = rsb("st", [P, 4, TILES])
            pexp = rsb("pexp", [P, TILES])
            gate = rsb("gate", [P, TILES, EXPERTS])
            work = rsb("work", [P, TILES, EXPERTS])
            rank = rsb("rank", [P, TILES, EXPERTS])
            mask = rsb("mask", [P, TILES, EXPERTS], BF16)
            pre = rsb("pre", [P, 2, 8 + TILES, EXPERTS], BF16)
            top = rsb("top", [P, TILES, TOPK])
            topi = rsb("topi", [P, TILES, TOPK], U32)
            topf = rsb("topf", [P, TILES, TOPK])
            hit = rsb("hit", [P, 2, TOPK, EXPERTS])
            rk = rsb("rk", [P, TILES, TOPK])
            sm = rsb("sm", [P, 3, TILES])
            far = rsb("far", [P, TILES, TOPK])
            pl = rsb("pl", [P, TILES, TOPK])
            pli = rsb("pli", [P, TILES * TOPK], I32)
            lo_i = rsb("lo_i", [P, 2, TILES * TOPK], I32)
            lo = rsb("lo", [P, 2, TILES, TOPK])
            rowc = rsb("rowc", [P, TILES, TOPK])
            cur = rsb("cur", [P, 2, 3, TOPK])
            oh_p = rsb("oh_p", [P, 2, TOPK, P], BF16)
            oh_c = rsb("oh_c", [P, 2, TOPK, 2 * COLS], BF16)
            tf = rsb("tf", [P, 6, COLS])
            ti = rsb("ti", [P, 4, COLS], I32)
            sil = rsb("sil", [P, 2, BLK])
            hid = rsb("hid", [P, 2, FC, BLK])
            shsb = rsb("shsb", [P, WCOLS])
            wgsb = rsb("wgsb", [P, EXPERTS])

            w_in = rsem("w_in")
            dv = rsem("dv")
            sqd = rsem("sqd")
            rstd = rsem("rstd")
            exped = rsem("exped")
            tps = rsem("tps")
            tsb = rsem("tsb")
            logit = rsem("logit")
            ranked = rsem("ranked")
            sh_h = rsem("sh_h")
            sh_c = rsem("sh_c")
            sh_a = rsem("sh_a")
            sh_o = rsem("sh_o")
            sh_x = rsem("sh_x")
            oh = rsem("oh")
            inv = rsem("inv")
            pconst = rsem("pconst")

            LOGB, RANKB, TRB, HB, OB, INVB = 0, 0, 2, 2, 6, 7
            OT = TILES // 2

            with nc.Block() as block:
                @block.sync
                def _(sp):
                    sp.dma_start(shsb[:, :], shw).then_inc(w_in, 16)
                    sp.dma_start(wgsb[:, :], wg).then_inc(w_in, 16)
                    for e in range(STEP_EXPERTS):
                        sp.dma_start(ring[:, e, :], wexp[e]).then_inc(w_landed[e], 16)
                    sp.wait_ge(dv, 6)
                    sp.dma_start(xn_dram.rearrange("(t p) d -> p t d", p=P), xn[:, :, :]).then_inc(xn_stored, 16)
                    y0 = ydram.rearrange("(c p r) d -> c p (r d)", p=P, r=TOPK)
                    for c in range(TILES):
                        sp.dma_start(y0[c], zeros[:, :]).then_inc(zeroed, 16)
                    sp.wait_ge(w_in, 32)

                @block.gpsimd
                def _(pool):
                    nc.gpsimd.memset(pexp[:, :], -0.5).then_inc(pconst, 1)
                    nc.gpsimd.memset(pre[:, :, 0:8, :], 0.0).then_inc(pconst, 1)
                    nc.gpsimd.iota(rowc[:, :, :].rearrange("p t k -> p (t k)"), [[1, TILES * TOPK]], base=0,
                                   channel_multiplier=0, allow_small_or_imprecise_dtypes=True).then_inc(pconst, 1)
                    pool.wait_ge(pconst, 1)
                    pool.wait_ge(dv, 5)
                    nc.gpsimd.tensor_tensor(st[:, 3, :], st[:, 2, :], pexp[:, :], ALU.pow).then_inc(rstd, 1)
                    for c in range(FC * BLOCKS):
                        b, f = c // FC, c % FC
                        pool.wait_ge(sh_c, c + 1)
                        nc.gpsimd.tensor_tensor(hid[:, b % 2, f, :], hid[:, b % 2, f, :], sil[:, c % 2, :],
                                                ALU.mult).then_inc(sh_a, 1)

                @block.vector
                def _(v):
                    n = [0]

                    def step(ins):
                        n[0] += 1
                        ins.then_inc(dv, 1)
                        v.wait_ge(dv, n[0])

                    def bc(ap, m):
                        return ap.unsqueeze(2).to_broadcast([P, TILES, m])

                    step(nc.vector.tensor_reduce(st[:, 0, :], x[:, :, :], AX.X, ALU.add))
                    step(nc.vector.tensor_scalar(st[:, 0, :], st[:, 0, :], 1.0 / DIM, None, ALU.mult))
                    step(nc.vector.tensor_tensor(xn[:, :, :], x[:, :, :], bc(st[:, 0, :], DIM), ALU.subtract))
                    v.wait_ge(sqd, 1)
                    step(nc.vector.tensor_reduce(st[:, 1, :], sq[:, :, :], AX.X, ALU.add))
                    step(nc.vector.tensor_scalar(st[:, 2, :], st[:, 1, :], 1.0 / DIM, EPS_LN, ALU.mult, ALU.add))
                    v.wait_ge(rstd, 1)
                    step(nc.vector.tensor_tensor(xn[:, :, :], xn[:, :, :], bc(st[:, 3, :], DIM), ALU.mult))
                    for c in range(BLOCKS):
                        v.wait_ge(tps, c + 1)
                        nc.vector.tensor_copy(xnT[:, c * BLK:(c + 1) * BLK], ps[:, TRB + c, :]).then_inc(tsb, 1)
                    v.wait_ge(logit, 1)
                    lg = ps[:, LOGB:LOGB + 2, :].rearrange("p b (t e) -> p (b t) e", e=EXPERTS)
                    step(nc.vector.tensor_reduce(sm[:, 0, :], lg, AX.X, ALU.max))
                    step(nc.vector.tensor_tensor(work[:, :, :], lg, bc(sm[:, 0, :], EXPERTS), ALU.subtract))
                    v.wait_ge(exped, 1)
                    step(nc.vector.tensor_reduce(sm[:, 1, :], gate[:, :, :], AX.X, ALU.add))
                    step(nc.vector.reciprocal(sm[:, 2, :], sm[:, 1, :]))
                    step(nc.vector.tensor_tensor(gate[:, :, :], gate[:, :, :], bc(sm[:, 2, :], EXPERTS), ALU.mult))
                    for t in range(TILES):
                        last = nc.vector.max(top[:, t, :], gate[:, t, :])
                    step(last)
                    for t in range(TILES):
                        last = nc.vector.max_index(topi[:, t, :], top[:, t, :], gate[:, t, :])
                    step(last)
                    for t in range(TILES):
                        last = nc.vector.match_replace(work[:, t, :], top[:, t, :], gate[:, t, :], -1.0)
                    step(last)
                    step(nc.vector.tensor_scalar(pre[:, 0, 8:, :], work[:, :, :], 0.0, None, ALU.is_lt))
                    nc.vector.tensor_copy(mask[:, :, :], pre[:, 0, 8:, :])
                    v.wait_ge(pconst, 2)
                    for i, s in enumerate((1, 2, 4, 8)):
                        a, b = i % 2, (i + 1) % 2
                        step(nc.vector.tensor_tensor(pre[:, b, 8:, :], pre[:, a, 8:, :],
                                                     pre[:, a, 8 - s:8 - s + TILES, :], ALU.add))
                    step(nc.vector.tensor_reduce(sm[:, 0, :], top[:, :, :], AX.X, ALU.add))
                    step(nc.vector.tensor_scalar(sm[:, 0, :], sm[:, 0, :], EPS_F32, None, ALU.max))
                    step(nc.vector.reciprocal(sm[:, 1, :], sm[:, 0, :]))
                    step(nc.vector.scalar_tensor_tensor(wk[:, :, :], top[:, :, :], 0.5, bc(sm[:, 1, :], TOPK),
                                                        ALU.mult, ALU.mult))
                    step(nc.vector.tensor_copy(topf[:, :, :], topi[:, :, :]))
                    v.wait_ge(ranked, 1)
                    step(nc.vector.tensor_copy(rank[:, :, :].rearrange("p t e -> p (t e)"),
                                               ps[:, RANKB:RANKB + 2, :].rearrange("p b c -> p (b c)")))
                    for t in range(TILES):
                        for k in range(TOPK):
                            last = nc.vector.scalar_tensor_tensor(
                                hit[:, t % 2, k, :], iota_e[:, :], topf[:, t, k:k + 1], rank[:, t, :],
                                ALU.is_equal, ALU.mult, accum_out=rk[:, t, k:k + 1])
                        n[0] += 1
                        last.then_inc(dv, 1)
                        v.wait_ge(dv, n[0] - 1 if t < TILES - 1 else n[0])
                    step(nc.vector.tensor_scalar(far[:, :, :], rk[:, :, :], CAPACITY - 0.5, FAR, ALU.is_gt, ALU.mult))
                    step(nc.vector.scalar_tensor_tensor(pl[:, :, :], topf[:, :, :], float(CAPACITY), rk[:, :, :],
                                                        ALU.mult, ALU.add))
                    step(nc.vector.tensor_tensor(pli[:, :], pl[:, :, :].rearrange("p t k -> p (t k)"),
                                                 far[:, :, :].rearrange("p t k -> p (t k)"), ALU.add))
                    nc.vector.tensor_scalar(lo_i[:, 0, :], pli[:, :], P - 1, None, ALU.bitwise_and)
                    step(nc.vector.tensor_scalar(lo_i[:, 1, :], pli[:, :], 7, None, ALU.logical_shift_right))
                    step(nc.vector.tensor_copy(lo[:, :, :, :].rearrange("p a t k -> p a (t k)"), lo_i[:, :, :]))
                    v.wait_ge(pconst, 3)
                    base = n[0]
                    with v.Fori(0, OT) as i:
                        for h in range(2):
                            v.wait_ge(inv, 2 * i + h + 1)
                            t = 2 * i + h
                            nc.vector.tensor_copy(cur[:, h, 0:2, :], lo[:, :, bass.ds(t, 1), :].rearrange("p a t k -> p a (t k)"))
                            nc.vector.tensor_copy(cur[:, h, 2, :], rowc[:, bass.ds(t, 1), :].rearrange("p t k -> p (t k)")).then_inc(dv, 1)
                            v.wait_ge(dv, base + 2 * i + h + 1)
                            for k in range(TOPK):
                                nc.vector.tensor_scalar(oh_p[:, h, k, :], iota_p[:, :], cur[:, h, 0, k:k + 1], None,
                                                        ALU.is_equal)
                                nc.vector.tensor_scalar(oh_c[:, h, k, 0:COLS], iota_c[:, :], cur[:, h, 1, k:k + 1],
                                                        tokp1[:, 0:1], ALU.is_equal, ALU.mult)
                                last = nc.vector.tensor_scalar(oh_c[:, h, k, COLS:], iota_c[:, :],
                                                               cur[:, h, 1, k:k + 1], cur[:, h, 2, k:k + 1],
                                                               ALU.is_equal, ALU.mult)
                            last.then_inc(oh, 1)
                    n[0] = base + TILES
                    v.wait_ge(inv, TILES + 2)
                    step(nc.vector.tensor_copy(tf[:, 0:2, :].rearrange("p a c -> p (a c)"), ps[:, INVB, 0:2 * COLS]))
                    step(nc.vector.tensor_copy(ti[:, 0, :], tf[:, 1, :]))
                    nc.vector.tensor_scalar(ti[:, 1, :], ti[:, 0, :], 3, None, ALU.logical_shift_right)
                    step(nc.vector.tensor_scalar(ti[:, 2, :], ti[:, 0, :], TOPK - 1, None, ALU.bitwise_and))
                    step(nc.vector.tensor_copy(tf[:, 2:4, :], ti[:, 1:3, :]))
                    step(nc.vector.scalar_tensor_tensor(tf[:, 4, :], tf[:, 2, :], float(P), tf[:, 0, :],
                                                        ALU.mult, ALU.add))
                    step(nc.vector.tensor_scalar(tf[:, 4, :], tf[:, 4, :], -1.0, None, ALU.add))
                    nc.vector.tensor_scalar(take[:, :], tf[:, 4, :], 0.0, None, ALU.max)
                    step(nc.vector.scalar_tensor_tensor(tf[:, 5, :], tf[:, 4, :], float(TOPK), tf[:, 3, :],
                                                        ALU.mult, ALU.add))
                    step(nc.vector.tensor_scalar(tf[:, 4, :], tf[:, 0, :], 0.5, FAR, ALU.is_lt, ALU.mult))
                    step(nc.vector.tensor_tensor(put[:, :], tf[:, 5, :], tf[:, 4, :], ALU.add))

                SUMMED = 19

                @block.tensor
                def _(pe):
                    nc.tensor.matmul(ps[:, INVB, 0:2 * COLS], zeros[:, 0:P // 2].bitcast(BF16),
                                     zeros[:, 0:COLS].bitcast(BF16), start=True, stop=True).then_inc(inv, 2)
                    pe.wait_ge(dv, 6)
                    for t in range(TILES):
                        mm = nc.tensor.transpose(ps[:, TRB + t // 4, (t % 4) * P:(t % 4 + 1) * P], xn[:, t, :],
                                                 ident[:, :])
                        if t % 4 == 3:
                            mm.then_inc(tps, 1)
                    pe.wait_ge(w_in, 32)
                    for t in range(TILES):
                        if t % 4 == 0:
                            pe.wait_ge(tsb, t // 4 + 1)
                        mm = nc.tensor.matmul(ps[:, LOGB + t // 8, (t % 8) * EXPERTS:(t % 8 + 1) * EXPERTS],
                                              xnT[:, t * P:(t + 1) * P], wgsb[:, :], start=True, stop=True)
                    mm.then_inc(logit, 1)

                    def up(c):
                        b, f, h = c // FC, c % FC, c % 2
                        if c == 0:
                            pe.wait_ge(tsb, BLOCKS)
                        if c >= 2:
                            pe.wait_ge(sh_c, c - 1)
                        for half in range(2):
                            mm = nc.tensor.matmul(ps[:, HB + 2 * h + half, :],
                                                  shsb[:, half * FFN + f * P:half * FFN + (f + 1) * P],
                                                  xnT[:, b * BLK:(b + 1) * BLK], start=True, stop=True)
                        mm.then_inc(sh_h, 1)

                    def down(b):
                        pe.wait_ge(sh_a, FC * (b + 1))
                        if b >= 1:
                            pe.wait_ge(sh_x, b)
                        for j in range(BLK // P):
                            for f in range(FC):
                                mm = nc.tensor.matmul(ps[:, OB, j * P:(j + 1) * P],
                                                      hid[:, b % 2, f, j * P:(j + 1) * P],
                                                      shsb[:, 2 * FFN + f * DIM:2 * FFN + (f + 1) * DIM],
                                                      start=(f == 0), stop=(f == FC - 1))
                        mm.then_inc(sh_o, 1)

                    def ranks():
                        pe.wait_ge(dv, SUMMED)
                        for t in range(TILES):
                            o = ps[:, RANKB + t // 8, (t % 8) * EXPERTS:(t % 8 + 1) * EXPERTS]
                            mm = nc.tensor.matmul(o, before[:, :], mask[:, t, :], start=True, stop=(t == 0))
                            if t:
                                mm = nc.tensor.matmul(o, ones_bf[:, :], pre[:, 0, 8 + t - 1, :],
                                                      start=False, stop=True)
                        mm.then_inc(ranked, 1)

                    for c in range(FC * BLOCKS):
                        up(c)
                        if c == 7:
                            ranks()
                        if c % FC == 0 and c:
                            down(c // FC - 1)
                    down(BLOCKS - 1)
                    with pe.Fori(0, OT) as i:
                        for h in range(2):
                            pe.wait_ge(oh, 2 * i + h + 1)
                            for k in range(TOPK):
                                mm = nc.tensor.matmul(ps[:, INVB, 0:2 * COLS], oh_p[:, h, k, :], oh_c[:, h, k, :],
                                                      start=False, stop=False, skip_group_check=True)
                            mm.then_inc(inv, 1)

                @block.scalar
                def _(act):
                    act.wait_ge(dv, 3)
                    nc.scalar.activation(sq[:, :, :], xn[:, :, :], ACT.Square).then_inc(sqd, 1)
                    act.wait_ge(dv, 8)
                    nc.scalar.activation(gate[:, :, :], work[:, :, :], ACT.Exp).then_inc(exped, 1)

                    def half_down(b):
                        act.wait_ge(sh_o, b + 1)
                        nc.scalar.mul(sq[:, b * 4:(b + 1) * 4, :].rearrange("p t d -> p (t d)"), ps[:, OB, :],
                                      0.5).then_inc(sh_x, 1)

                    act.wait_ge(dv, 4)
                    for c in range(FC * BLOCKS):
                        b, f = c // FC, c % FC
                        act.wait_ge(sh_h, c + 1)
                        if c >= 2:
                            act.wait_ge(sh_a, c - 1)
                        nc.scalar.activation(sil[:, c % 2, :], ps[:, HB + 2 * (c % 2) + 1, :], ACT.Silu)
                        if b >= 2:
                            act.wait_ge(sh_o, b - 1)
                        nc.scalar.copy(hid[:, b % 2, f, :], ps[:, HB + 2 * (c % 2), :]).then_inc(sh_c, 1)
                        if c % FC == FC - 1 and b >= 1:
                            half_down(b - 1)
                    half_down(BLOCKS - 1)

        with ExitStack() as ectx:
            def esb(name, shape, dt=F32):
                return ectx.enter_context(nc.sbuf_tensor(f"{tag}_{name}", shape, dt))

            def esem(name):
                return ectx.enter_context(nc.semaphore(f"{tag}_{name}"))

            SG = STEP_GROUPS
            tk = esb("tk", [P, SG, GT], I32)
            pt = esb("pt", [P, SG, GT], I32)
            xg = esb("xg", [P, SG, GT, DIM])
            xgT = esb("xgT", [P, SG, GW])
            sil = esb("esil", [P, 2, FC * CAPACITY])
            hid = esb("ehid", [P, 2, FC * CAPACITY])
            oT = esb("oT", [P, SG, GW])
            og = esb("og", [P, SG, GT, DIM])

            passed = esem("passed")
            tk_in = esem("tk_in")
            pt_in = esem("pt_in")
            got = [[esem(f"got{g}_{s}") for s in range(GT)] for g in range(SG)]
            sent = [[esem(f"sent{g}_{s}") for s in range(GT)] for g in range(SG)]
            xg_t = esem("xg_t")
            xg_s = esem("xg_s")
            hb = esem("hb")
            sl = esem("sl")
            ac = esem("ac")
            ob = esem("ob")
            os_ = esem("os")
            og_t = esem("og_t")
            og_s = esem("og_s")
            XB, HB, OB, GB = 0, 2, 6, 7

            with nc.Block() as block:
                @block.sync
                def _(sp):
                    with sp.Fori(1, STEPS) as i:
                        for e in range(STEP_EXPERTS):
                            sp.wait_ge(ob, STEP_EXPERTS * (i - 1) + e + 1)
                            sp.dma_start(ring[:, e, :], wexp[bass.ds(STEP_EXPERTS * i + e, 1), :, :].rearrange(
                                "e p c -> (e p) c")).then_inc(w_landed[e], 16)

                @block.gpsimd
                def _(pool):
                    def gather(i, g):
                        G = SG * i + g
                        after(pool, xg_t, G - 1)
                        pool.wait_ge(xn_stored, 16)
                        nc.gpsimd.tensor_copy(tk[:, g, :], take[:, bass.ds(G * GT, GT)]).then_inc(tk_in, 1)
                        pool.wait_ge(tk_in, G + 1)
                        pool.sem_inc(passed, 1)
                        for s in range(GT):
                            nc.gpsimd.indirect_dma_start(
                                xg[:, g, s, :], None, xn_dram, bass.IndirectOffsetOnAxis(tk[:, g, s:s + 1], 0),
                                bounds_check=TOKENS - 1, oob_is_err=False).then_inc(got[g][s], 16)

                    def scatter(i, g):
                        G = SG * i + g
                        for s in range(GT):
                            after(pool, sent[g][s], 16 * i)
                        pool.wait_ge(zeroed, 16 * TILES)
                        nc.gpsimd.tensor_copy(pt[:, g, :], put[:, bass.ds(G * GT, GT)]).then_inc(pt_in, 1)
                        pool.wait_ge(pt_in, G + 1)
                        pool.wait_ge(og_s, 2 * G + 2)
                        pool.sem_inc(passed, 1)
                        for s in range(GT):
                            nc.gpsimd.indirect_dma_start(
                                ydram, bass.IndirectOffsetOnAxis(pt[:, g, s:s + 1], 0), og[:, g, s, :], None,
                                bounds_check=YROWS - 1, oob_is_err=False).then_inc(sent[g][s], 16)

                    for g in range(SG):
                        gather(0, g)
                    for g in range(SG):
                        gather(1, g)
                        scatter(0, g)
                    with pool.Fori(2, STEPS) as i:
                        for g in range(SG):
                            gather(i, g)
                            scatter(i - 1, g)
                    for g in range(SG):
                        scatter(STEPS - 1, g)
                    for g in range(SG):
                        for s in range(GT):
                            pool.wait_ge(sent[g][s], 16 * STEPS)

                @block.tensor
                def _(pe):
                    def turn_in(i, g):
                        G = SG * i + g
                        after(pe, xg_s, G)
                        for s in range(GT):
                            pe.wait_ge(got[g][s], 16 * i + 16)
                            mm = nc.tensor.transpose(ps[:, XB + s // 4, (s % 4) * P:(s % 4 + 1) * P],
                                                     xg[:, g, s, :], ident[:, :])
                        mm.then_inc(xg_t, 1)

                    def up(i, e):
                        g, E = e // GE, STEP_EXPERTS * i + e
                        pe.wait_ge(w_landed[e], 16 * i + 16)
                        if e % GE == 0:
                            pe.wait_ge(xg_s, SG * i + g + 1)
                        after(pe, ac, E - 1)
                        a = (e % GE) * CAPACITY
                        for half in range(2):
                            for f in range(FC):
                                mm = nc.tensor.matmul(
                                    ps[:, HB + 2 * (e % 2) + half, f * CAPACITY:(f + 1) * CAPACITY],
                                    ring[:, e, half * FFN + f * P:half * FFN + (f + 1) * P],
                                    xgT[:, g, a:a + CAPACITY], start=True, stop=True)
                        mm.then_inc(hb, 1)

                    def down(i, e):
                        E = STEP_EXPERTS * i + e
                        pe.wait_ge(ac, E + 1)
                        after(pe, os_, E)
                        for f in range(FC):
                            mm = nc.tensor.matmul(ps[:, OB, 0:CAPACITY],
                                                  ring[:, e, 2 * FFN + f * DIM:2 * FFN + (f + 1) * DIM],
                                                  hid[:, e % 2, f * CAPACITY:(f + 1) * CAPACITY],
                                                  start=(f == 0), stop=(f == FC - 1))
                        mm.then_inc(ob, 1)

                    def turn_out(i, g, part):
                        G = SG * i + g
                        pe.wait_ge(os_, GE * (G + 1))
                        after(pe, og_s, 2 * G + part)
                        for s in range(3) if part == 0 else range(3, GT):
                            mm = nc.tensor.transpose(ps[:, GB, (s % 3) * P:(s % 3 + 1) * P],
                                                     oT[:, g, s * P:(s + 1) * P], ident[:, :])
                        mm.then_inc(og_t, 1)

                    def step(i, first, last):
                        for e in range(STEP_EXPERTS):
                            g, r = e // GE, e % GE
                            if r == 2 and not (last and g == SG - 1):
                                turn_in(*((i, g + 1) if g < SG - 1 else (i + 1, 0)))
                            if e < STEP_EXPERTS - 1:
                                up(i, e + 1)
                            elif not last:
                                up(i + 1, 0)
                            down(i, e)
                            if r in (0, 1) and not (first and g == 0):
                                turn_out(*((i, g - 1) if g else (i - 1, SG - 1)), r)

                    turn_in(0, 0)
                    up(0, 0)
                    step(0, True, False)
                    step(1, False, False)
                    with pe.Fori(2, STEPS - 1) as i:
                        step(i, False, False)
                    step(STEPS - 1, False, True)
                    turn_out(STEPS - 1, SG - 1, 0)
                    turn_out(STEPS - 1, SG - 1, 1)

                @block.scalar
                def _(act):
                    def group_in(i, g):
                        G = SG * i + g
                        act.wait_ge(xg_t, G + 1)
                        after(act, hb, GE * (G - 1))
                        nc.scalar.copy(xgT[:, g, :], ps[:, XB:XB + 2, :].rearrange("p b c -> p (b c)")[:, 0:GW]
                                       ).then_inc(xg_s, 1)

                    def silu(i, e):
                        E = STEP_EXPERTS * i + e
                        act.wait_ge(hb, E + 1)
                        after(act, ac, E - 1)
                        nc.scalar.activation(sil[:, e % 2, :], ps[:, HB + 2 * (e % 2) + 1, 0:FC * CAPACITY],
                                             ACT.Silu).then_inc(sl, 1)

                    def group_out(i, g, part):
                        G = SG * i + g
                        act.wait_ge(og_t, 2 * G + part + 1)
                        if part == 0:
                            for s in range(GT):
                                after(act, sent[g][s], 16 * i)
                        a, b = ((0, 3), (3, GT))[part]
                        nc.scalar.copy(og[:, g, a:b, :].rearrange("p s d -> p (s d)"),
                                       ps[:, GB, 0:(b - a) * P]).then_inc(og_s, 1)

                    def step(i, first, last):
                        for e in range(STEP_EXPERTS):
                            g, r = e // GE, e % GE
                            if r == 2 and not (last and g == SG - 1):
                                group_in(*((i, g + 1) if g < SG - 1 else (i + 1, 0)))
                            if e < STEP_EXPERTS - 1:
                                silu(i, e + 1)
                            elif not last:
                                silu(i + 1, 0)
                            if r in (0, 1) and not (first and g == 0):
                                group_out(*((i, g - 1) if g else (i - 1, SG - 1)), r)

                    group_in(0, 0)
                    silu(0, 0)
                    step(0, True, False)
                    step(1, False, False)
                    with act.Fori(2, STEPS - 1) as i:
                        step(i, False, False)
                    step(STEPS - 1, False, True)
                    group_out(STEPS - 1, SG - 1, 0)
                    group_out(STEPS - 1, SG - 1, 1)

                @block.vector
                def _(v):
                    nc.vector.tensor_tensor(x[:, :, :], x[:, :, :], half_shared[:, :, :], ALU.add)

                    def product(i, e):
                        E = STEP_EXPERTS * i + e
                        v.wait_ge(sl, E + 1)
                        after(v, ob, E - 1)
                        nc.vector.tensor_tensor(hid[:, e % 2, :], sil[:, e % 2, :],
                                                ps[:, HB + 2 * (e % 2), 0:FC * CAPACITY], ALU.mult).then_inc(ac, 1)

                    def output(i, e):
                        g, E = e // GE, STEP_EXPERTS * i + e
                        v.wait_ge(ob, E + 1)
                        if e % GE == 0:
                            after(v, og_t, 2 * (SG * i + g - 1))
                        a = (e % GE) * CAPACITY
                        nc.vector.tensor_copy(oT[:, g, a:a + CAPACITY], ps[:, OB, 0:CAPACITY]).then_inc(os_, 1)

                    def step(i, first, last):
                        for e in range(STEP_EXPERTS):
                            if e < STEP_EXPERTS - 1:
                                product(i, e + 1)
                            elif not last:
                                product(i + 1, 0)
                            output(i, e)

                    product(0, 0)
                    step(0, True, False)
                    step(1, False, False)
                    with v.Fori(2, STEPS - 1) as i:
                        step(i, False, False)
                    step(STEPS - 1, False, True)

        with ExitStack() as cctx:
            YB = 4
            yt = cctx.enter_context(nc.sbuf_tensor(f"{tag}_yt", [P, 2, YB, TOPK * DIM], F32))
            y_in = [cctx.enter_context(nc.semaphore(f"{tag}_y_in{q}")) for q in range(2)]
            summed = cctx.enter_context(nc.semaphore(f"{tag}_summed"))
            stored = cctx.enter_context(nc.semaphore(f"{tag}_stored"))
            ysrc = ydram.rearrange("(c p r) d -> c p (r d)", p=P, r=TOPK)
            QS = TILES // YB
            with nc.Block() as block:
                @block.sync
                def _(sp):
                    for q in range(QS):
                        if q >= 2:
                            sp.wait_ge(summed, TOPK * (q - 1))
                        sp.dma_start(yt[:, q % 2, :, :], ysrc[q * YB:(q + 1) * YB].rearrange("c p w -> p c w")
                                     ).then_inc(y_in[q % 2], 16)
                    if out_dram is not None:
                        dst = out_dram.rearrange("(t p) d -> p t d", p=P)
                        for q in range(QS):
                            sp.wait_ge(summed, TOPK * (q + 1))
                            sp.dma_start(dst[:, q * YB:(q + 1) * YB, :], x[:, q * YB:(q + 1) * YB, :]
                                         ).then_inc(stored, 16)
                        sp.wait_ge(stored, 16 * QS)

                @block.vector
                def _(v):
                    n = 0
                    for q in range(QS):
                        v.wait_ge(y_in[q % 2], 16 * (q // 2 + 1))
                        for k in range(TOPK):
                            if k:
                                v.wait_ge(summed, n)
                            for j in range(YB):
                                t = q * YB + j
                                last = nc.vector.scalar_tensor_tensor(
                                    x[:, t, :], yt[:, q % 2, j, k * DIM:(k + 1) * DIM], wk[:, t, k:k + 1],
                                    x[:, t, :], ALU.mult, ALU.add)
                            n += 1
                            last.then_inc(summed, 1)



def attention(nc, x, attn_w, consts, ps):
    wqkv, wout, wf, bf, bo, tabs, four = attn_w
    ident = consts[0]
    with ExitStack() as ctx:
        def sb(name, shape, dt=F32):
            return ctx.enter_context(nc.sbuf_tensor(f"at_{name}", shape, dt))

        def sem(name):
            return ctx.enter_context(nc.semaphore(f"at_{name}"))

        QKW = 2 * P
        wq_sb = sb("wqkv", [P, PAIRS, 3 * P])
        wo_sb = sb("wout", [P, PAIRS, DIM])
        wf_sb = sb("wf", [2 * FREQS, P])
        four_sb = sb("four", [2 * FREQS, SEQ])
        bf_sb = sb("bf", [P, 1])
        bo_sb = sb("bo", [P, DIM])
        cos = sb("cos", [P, TPB, DH])
        sin = sb("sin", [P, TPB, DH])
        fenc = sb("fenc", [P, SEQ])
        fencs = sb("fencs", [P, SEQ])
        xall = sb("xall", [P, TOKENS])
        xcur = sb("xcur", [P, SEQ])
        xnext = sb("xnext", [P, SEQ])

        loaded = sem("loaded")
        ready = sem("ready")
        with ExitStack() as lctx:
            xn = lctx.enter_context(nc.sbuf_tensor("at_xn", [P, TILES, DIM], F32))
            sq = lctx.enter_context(nc.sbuf_tensor("at_sq", [P, TILES, DIM], F32))
            st = lctx.enter_context(nc.sbuf_tensor("at_st", [P, 4, TILES], F32))
            pexp = lctx.enter_context(nc.sbuf_tensor("at_pexp", [P, TILES], F32))
            dv, sqd, rstd, tps, fe = (lctx.enter_context(nc.semaphore(f"at_{q}"))
                                      for q in ("dv", "sqd", "rstd", "tps", "fe"))
            with nc.Block() as block:
                @block.sync
                def _(sp):
                    for dst, src in ((wq_sb[:, :, :], wqkv), (wo_sb[:, :, :], wout), (wf_sb[:, :], wf),
                                     (four_sb[:, :], four), (bf_sb[:, :], bf), (bo_sb[:, :], bo),
                                     (cos[:, :, :], tabs[0]), (sin[:, :, :], tabs[1])):
                        sp.dma_start(dst, src).then_inc(loaded, 16)
                    sp.wait_ge(loaded, 128)

                @block.gpsimd
                def _(pool):
                    nc.gpsimd.memset(pexp[:, :], -0.5).then_inc(ready, 1)
                    pool.wait_ge(ready, 1)
                    pool.wait_ge(dv, 5)
                    nc.gpsimd.tensor_tensor(st[:, 3, :], st[:, 2, :], pexp[:, :], ALU.pow).then_inc(rstd, 1)

                @block.vector
                def _(v):
                    n = [0]

                    def step(ins):
                        n[0] += 1
                        ins.then_inc(dv, 1)
                        v.wait_ge(dv, n[0])

                    def bc(ap):
                        return ap.unsqueeze(2).to_broadcast([P, TILES, DIM])

                    step(nc.vector.tensor_reduce(st[:, 0, :], x[:, :, :], AX.X, ALU.add))
                    step(nc.vector.tensor_scalar(st[:, 0, :], st[:, 0, :], 1.0 / DIM, None, ALU.mult))
                    step(nc.vector.tensor_tensor(xn[:, :, :], x[:, :, :], bc(st[:, 0, :]), ALU.subtract))
                    v.wait_ge(sqd, 1)
                    step(nc.vector.tensor_reduce(st[:, 1, :], sq[:, :, :], AX.X, ALU.add))
                    step(nc.vector.tensor_scalar(st[:, 2, :], st[:, 1, :], 1.0 / DIM, EPS_LN, ALU.mult, ALU.add))
                    v.wait_ge(rstd, 1)
                    step(nc.vector.tensor_tensor(xn[:, :, :], xn[:, :, :], bc(st[:, 3, :]), ALU.mult))
                    v.wait_ge(loaded, 128)
                    nc.vector.tensor_tensor(x[:, :, :], x[:, :, :],
                                            bo_sb[:, :].unsqueeze(1).to_broadcast([P, TILES, DIM]), ALU.add)
                    v.wait_ge(fe, 1)
                    step(nc.vector.tensor_scalar(fenc[:, :], ps[:, 0, 0:SEQ], bf_sb[:, 0:1], None, ALU.add))
                    step(nc.vector.tensor_scalar(fencs[:, :], fenc[:, :], SCALE, None, ALU.mult))
                    for c in range(BLOCKS):
                        v.wait_ge(tps, c + 1)
                        nc.vector.tensor_copy(xall[:, c * BLK:(c + 1) * BLK], ps[:, 2 + c, :])

                @block.scalar
                def _(act):
                    act.wait_ge(dv, 3)
                    nc.scalar.activation(sq[:, :, :], xn[:, :, :], ACT.Square).then_inc(sqd, 1)

                @block.tensor
                def _(pe):
                    pe.wait_ge(loaded, 128)
                    nc.tensor.matmul(ps[:, 0, 0:SEQ], wf_sb[:, :], four_sb[:, :], start=True,
                                     stop=True).then_inc(fe, 1)
                    pe.wait_ge(dv, 6)
                    for t in range(TILES):
                        mm = nc.tensor.transpose(ps[:, 2 + t // 4, (t % 4) * P:(t % 4 + 1) * P], xn[:, t, :],
                                                 ident[:, :])
                        if t % 4 == 3:
                            mm.then_inc(tps, 1)

        m1 = sb("m1", [P, 2, TPB * QKW])
        m2 = sb("m2", [P, 2, TPB * QKW])
        vsb = sb("v", [P, 4, TPB, P])
        qT = sb("qT", [P, 2, SEQ])
        kT = sb("kT", [P, 2, 2, SEQ])
        nmax = sb("nmax", [P, 2, 2, TPB])
        rsum = sb("rsum", [P, 2, 2, TPB])
        rinv = sb("rinv", [P, 2, 2, TPB])
        prob = sb("prob", [P, 2, 2, TPB, SEQ])
        pT = sb("pT", [P, 2, TPB, SEQ])
        oT = sb("oTh", [P, PAIRS, SEQ])

        passed = sem("passed")
        xc, xx = sem("xc"), sem("xx")
        qk, vp, rope, vev, msum, tq, kev = (sem(q) for q in ("qk", "vp", "rope", "vev", "msum", "tq", "kev"))
        sc, mx, ex, rc, pn, pt, pte, pv, oev, op, res, z = (
            sem(q) for q in ("sc", "mx", "ex", "rc", "pn", "pt", "pte", "pv", "oev", "op", "res", "z"))
        QB, VB, TB, SB, PB, OB = 0, 1, 2, 3, 5, 7

        with nc.Block() as block:
            @block.gpsimd
            def _(pool):
                nc.gpsimd.memset(kT[:, :, :, :], 0.0).then_inc(z, 1)

                def load_cur(b):
                    after(pool, vp, PAIRS * b)
                    pool.sem_inc(passed, 1)
                    nc.gpsimd.tensor_copy(xcur[:, :], xall[:, bass.ds(b * SEQ, SEQ)]).then_inc(xc, 1)

                def load_next(b):
                    after(pool, vp, PAIRS * (b - 1) + 2)
                    pool.sem_inc(passed, 1)
                    nc.gpsimd.tensor_copy(xnext[:, :], xall[:, bass.ds(b * SEQ, SEQ)]).then_inc(xx, 1)

                def add(b, p):
                    u = PAIRS * b + p
                    pool.wait_ge(rope, u + 1)
                    after(pool, tq, u - 1)
                    nc.gpsimd.tensor_tensor(m1[:, p % 2, :], m1[:, p % 2, :], m2[:, p % 2, :],
                                            ALU.add).then_inc(msum, 1)

                def batch(b, last):
                    for p in range(PAIRS):
                        if p == 1 and not last:
                            load_next(b + 1)
                        if p + 2 < PAIRS:
                            add(b, p + 2)
                        elif not last:
                            if p == PAIRS - 2:
                                load_cur(b + 1)
                            add(b + 1, p + 2 - PAIRS)

                load_cur(0)
                add(0, 0)
                add(0, 1)
                batch(0, False)
                with pool.Fori(1, BATCH - 1) as b:
                    batch(b, False)
                batch(BATCH - 1, True)

            @block.tensor
            def _(pe):
                def qkv(b, p, xs):
                    u = PAIRS * b + p
                    after(pe, rope, u)
                    for t in range(TPB):
                        mm = nc.tensor.matmul(ps[:, QB, t * QKW:(t + 1) * QKW], xs[:, t * P:(t + 1) * P],
                                              wq_sb[:, p, 0:QKW], start=True, stop=True)
                    mm.then_inc(qk, 1)
                    after(pe, vev, u)
                    for t in range(TPB):
                        mm = nc.tensor.matmul(ps[:, VB, t * P:(t + 1) * P], xs[:, t * P:(t + 1) * P],
                                              wq_sb[:, p, QKW:], start=True, stop=True)
                    mm.then_inc(vp, 1)

                def turn(b, p):
                    u = PAIRS * b + p
                    pe.wait_ge(msum, u + 1)
                    after(pe, kev, u)
                    for half in range(2):
                        for t in range(TPB):
                            mm = nc.tensor.transpose(ps[:, TB, half * SEQ + t * P:half * SEQ + (t + 1) * P],
                                                     m1[:, p % 2, t * QKW + half * P:t * QKW + (half + 1) * P],
                                                     ident[:, :])
                    mm.then_inc(tq, 1)

                def scores(b, p, h):
                    u = PAIRS * b + p
                    if h == 0:
                        pe.wait_ge(kev, u + 1)
                    after(pe, ex, 2 * u + h - 1)
                    for t in range(TPB):
                        mm = nc.tensor.matmul(ps[:, SB + h, t * SEQ:(t + 1) * SEQ], qT[:, p % 2, t * P:(t + 1) * P],
                                              kT[:, p % 2, h, :], start=True, stop=True)
                    mm.then_inc(sc, 1)

                def turn_p(b, p, h):
                    u = PAIRS * b + p
                    pe.wait_ge(pn, 2 * u + h + 1)
                    after(pe, pte, 2 * u + h - 1)
                    for t in range(TPB):
                        for j in range(TPB):
                            mm = nc.tensor.transpose(ps[:, PB + h, j * SEQ + t * P:j * SEQ + (t + 1) * P],
                                                     prob[:, p % 2, h, t, j * P:(j + 1) * P], ident[:, :])
                    mm.then_inc(pt, 1)

                def values(b, p, h):
                    u = PAIRS * b + p
                    pe.wait_ge(pte, 2 * u + h + 1)
                    if h == 0:
                        pe.wait_ge(vev, u + 1)
                        after(pe, oev, u)
                    for j in range(TPB):
                        mm = nc.tensor.matmul(ps[h * DH:(h + 1) * DH, OB, 0:SEQ],
                                              vsb[:, p % 4, j, h * DH:(h + 1) * DH], pT[:, h, j, :],
                                              start=(j == 0), stop=(j == TPB - 1))
                    mm.then_inc(pv, 1)

                def project(b):
                    pe.wait_ge(oev, PAIRS * (b + 1))
                    for t in range(TPB):
                        for p in range(PAIRS):
                            mm = nc.tensor.matmul(ps[:, OB, t * DIM:(t + 1) * DIM], oT[:, p, t * P:(t + 1) * P],
                                                  wo_sb[:, p, :], start=(p == 0), stop=(p == PAIRS - 1))
                    mm.then_inc(op, 1)

                def batch(b, first, last):
                    for p in range(PAIRS):
                        bp, pp = (b, p - 1) if p else (b - 1, PAIRS - 1)
                        before = not (first and p == 0)
                        scores(b, p, 0)
                        scores(b, p, 1)
                        if p == 1 and not first:
                            project(b - 1)
                        if before:
                            turn_p(bp, pp, 0)
                        if p + 2 < PAIRS:
                            qkv(b, p + 2, xcur)
                        elif not last:
                            if p + 2 == PAIRS:
                                pe.wait_ge(xx, b + 1)
                            qkv(b + 1, p + 2 - PAIRS, xnext)
                        if before:
                            turn_p(bp, pp, 1)
                            if p == 1 and not first:
                                pe.wait_ge(res, b)
                            values(bp, pp, 0)
                        if p + 1 < PAIRS:
                            turn(b, p + 1)
                        elif not last:
                            turn(b + 1, 0)
                        if before:
                            values(bp, pp, 1)
                        if p == PAIRS - 1 and not last:
                            pe.wait_ge(xc, b + 2)

                pe.wait_ge(xc, 1)
                qkv(0, 0, xcur)
                qkv(0, 1, xcur)
                turn(0, 0)
                batch(0, True, False)
                with pe.Fori(1, BATCH - 1) as b:
                    batch(b, False, False)
                batch(BATCH - 1, False, True)
                for h in range(2):
                    turn_p(BATCH - 1, PAIRS - 1, h)
                for h in range(2):
                    values(BATCH - 1, PAIRS - 1, h)
                project(BATCH - 1)

            @block.vector
            def _(v):
                def rotate(b, p):
                    u = PAIRS * b + p
                    v.wait_ge(qk, u + 1)
                    after(v, tq, u - 1)
                    def tab(a, m):
                        return a.unsqueeze(2).to_broadcast([P, TPB, 4, DH]) if m else a
                    q = ps[:, QB, :].rearrange("p (t h d) -> p t h d", t=TPB, h=4)
                    for t in range(TPB):
                        nc.vector.tensor_tensor(
                            m1[:, p % 2, t * QKW:(t + 1) * QKW].rearrange("p (h d) -> p h d", h=4), q[:, t],
                            cos[:, t, :].unsqueeze(1).to_broadcast([P, 4, DH]), ALU.mult)
                        r = ps[:, QB, t * QKW:(t + 1) * QKW].rearrange("p (h i s) -> p h s i", h=4, s=2)
                        mm = nc.vector.tensor_tensor(
                            m2[:, p % 2, t * QKW:(t + 1) * QKW].rearrange("p (h s i) -> p h s i", h=4, s=2),
                            r[:, :, ::-1, :],
                            sin[:, t, :].rearrange("p (s i) -> p s i", s=2).unsqueeze(1).to_broadcast(
                                [P, 4, 2, DH // 2]), ALU.mult)
                    mm.then_inc(rope, 1)

                def take_k(b, p):
                    u = PAIRS * b + p
                    v.wait_ge(tq, u + 1)
                    after(v, sc, 2 * (u - 1))
                    for h in range(2):
                        r = slice(h * DH, (h + 1) * DH)
                        mm = nc.vector.tensor_tensor(kT[r, p % 2, h, :], ps[r, TB, SEQ:], fenc[r, :], ALU.add)
                    mm = nc.vector.scalar_tensor_tensor(qT[:, p % 2, :], ps[:, TB, 0:SEQ], SCALE, fencs[:, :],
                                                        ALU.mult, ALU.add)
                    mm.then_inc(kev, 1)

                def maximum(b, p, h):
                    u = PAIRS * b + p
                    v.wait_ge(sc, 2 * u + h + 1)
                    nc.vector.tensor_reduce(nmax[:, p % 2, h, :], ps[:, SB + h, :].rearrange("p (t k) -> p t k", t=TPB),
                                            AX.X, ALU.max, negate=True).then_inc(mx, 1)

                def normalise(b, p, h):
                    u = PAIRS * b + p
                    v.wait_ge(ex, 2 * u + h + 1)
                    nc.vector.reciprocal(rinv[:, p % 2, h, :], rsum[:, p % 2, h, :]).then_inc(rc, 1)
                    v.wait_ge(rc, 2 * u + h + 1)
                    for t in range(TPB):
                        mm = nc.vector.tensor_scalar(prob[:, p % 2, h, t, :], prob[:, p % 2, h, t, :],
                                                     rinv[:, p % 2, h, t:t + 1], None, ALU.mult)
                    mm.then_inc(pn, 1)

                def residual(b):
                    v.wait_ge(op, b + 1)
                    xs = x[:, bass.ds(TPB * b, TPB), :]
                    nc.vector.tensor_tensor(xs, ps[:, OB, 0:SEQ].rearrange("p (t d) -> p t d", t=TPB), xs,
                                            ALU.add).then_inc(res, 1)

                def batch(b, first, last):
                    for p in range(PAIRS):
                        maximum(b, p, 0)
                        maximum(b, p, 1)
                        if p == 1 and not first:
                            residual(b - 1)
                        normalise(b, p, 0)
                        if p + 2 < PAIRS:
                            rotate(b, p + 2)
                        elif not last:
                            rotate(b + 1, p + 2 - PAIRS)
                        if p + 1 < PAIRS:
                            take_k(b, p + 1)
                        elif not last:
                            take_k(b + 1, 0)
                        normalise(b, p, 1)

                v.wait_ge(z, 1)
                rotate(0, 0)
                rotate(0, 1)
                take_k(0, 0)
                batch(0, True, False)
                with v.Fori(1, BATCH - 1) as b:
                    batch(b, False, False)
                batch(BATCH - 1, False, True)
                residual(BATCH - 1)

            @block.scalar
            def _(act):
                def take_v(b, p):
                    u = PAIRS * b + p
                    act.wait_ge(vp, u + 1)
                    after(act, pv, 2 * (u - 3))
                    nc.scalar.copy(vsb[:, p % 4, :, :].rearrange("p t d -> p (t d)"), ps[:, VB, 0:TPB * P]
                                   ).then_inc(vev, 1)

                def exps(b, p, h):
                    u = PAIRS * b + p
                    act.wait_ge(mx, 2 * u + h + 1)
                    after(act, pt, 2 * (u - 2) + h + 1)
                    for t in range(TPB):
                        mm = nc.scalar.activation(prob[:, p % 2, h, t, :], ps[:, SB + h, t * SEQ:(t + 1) * SEQ],
                                                  ACT.Exp, bias=nmax[:, p % 2, h, t:t + 1],
                                                  accum_out=rsum[:, p % 2, h, t:t + 1])
                    mm.then_inc(ex, 1)

                def take_p(b, p, h):
                    u = PAIRS * b + p
                    act.wait_ge(pt, 2 * u + h + 1)
                    after(act, pv, 2 * (u - 1) + h + 1)
                    nc.scalar.copy(pT[:, h, :, :].rearrange("p j q -> p (j q)"), ps[:, PB + h, :]).then_inc(pte, 1)

                def take_o(b, p):
                    u = PAIRS * b + p
                    act.wait_ge(pv, 2 * u + 2)
                    if p == 0:
                        after(act, op, b)
                    nc.scalar.copy(oT[:, p, :], ps[:, OB, 0:SEQ]).then_inc(oev, 1)

                def batch(b, first, last):
                    for p in range(PAIRS):
                        bp, pp = (b, p - 1) if p else (b - 1, PAIRS - 1)
                        before = not (first and p == 0)
                        exps(b, p, 0)
                        if before:
                            take_p(bp, pp, 0)
                            take_p(bp, pp, 1)
                        exps(b, p, 1)
                        if p + 2 < PAIRS:
                            take_v(b, p + 2)
                        elif not last:
                            take_v(b + 1, p + 2 - PAIRS)
                        if before:
                            take_o(bp, pp)

                take_v(0, 0)
                take_v(0, 1)
                batch(0, True, False)
                with act.Fori(1, BATCH - 1) as b:
                    batch(b, False, False)
                batch(BATCH - 1, False, True)
                for h in range(2):
                    take_p(BATCH - 1, PAIRS - 1, h)
                take_o(BATCH - 1, PAIRS - 1)


def build(nc, t, out):
    with ExitStack() as ctx:
        def sb(name, shape, dt=F32):
            return ctx.enter_context(nc.sbuf_tensor(name, shape, dt))

        ps = ctx.enter_context(nc.psum_tensor("ps", [P, 8, BLK], F32))
        x = sb("x", [P, TILES, DIM])
        ident = sb("ident", [P, P])
        iota_e = sb("iota_e", [P, EXPERTS])
        iota_p = sb("iota_p", [P, P], BF16)
        iota_c = sb("iota_c", [P, COLS], BF16)
        before = sb("before", [P, P], BF16)
        ones_bf = sb("ones_bf", [P, P], BF16)
        tokp1 = sb("tokp1", [P, 1])
        zeros = sb("zeros", [P, TOPK * DIM])
        xn_dram = nc.dram_tensor("xn_rows", [TOKENS, DIM], F32, kind="Internal").ap()
        y_dram = [nc.dram_tensor(f"y_rows{i}", [YROWS, DIM], F32, kind="Internal").ap() for i in range(2)]
        x_in = ctx.enter_context(nc.semaphore("x_in"))
        c0 = ctx.enter_context(nc.semaphore("c0"))
        with nc.Block() as block:
            @block.sync
            def _(sp):
                sp.dma_start(x[:, :, :], t["x"].rearrange("(t p) d -> p t d", p=P)).then_inc(x_in, 16)
                sp.wait_ge(x_in, 16)

            @block.vector
            def _(v):
                nc.vector.memset(zeros[:, :], 0.0)
                nc.vector.memset(ones_bf[:, :], 1.0)

            @block.gpsimd
            def _(pool):
                nc.gpsimd.memset(ident[:, :], 1.0).then_inc(c0, 1)
                nc.gpsimd.memset(before[:, :], 1.0).then_inc(c0, 1)
                nc.gpsimd.iota(iota_e[:, :], [[1, EXPERTS]], base=0, channel_multiplier=0,
                               allow_small_or_imprecise_dtypes=True)
                nc.gpsimd.iota(iota_p[:, :], [[1, P]], base=0, channel_multiplier=0,
                               allow_small_or_imprecise_dtypes=True)
                nc.gpsimd.iota(iota_c[:, :], [[1, COLS]], base=0, channel_multiplier=0,
                               allow_small_or_imprecise_dtypes=True)
                nc.gpsimd.iota(tokp1[:, :], [[1, 1]], base=1, channel_multiplier=1,
                               allow_small_or_imprecise_dtypes=True)
                pool.wait_ge(c0, 2)
                nc.gpsimd.affine_select(out=ident[:, :], in_=ident[:, :], compare_op=ALU.is_equal, fill=0.0, base=0,
                                        pattern=[[-1, P]], channel_multiplier=1)
                nc.gpsimd.affine_select(out=before[:, :], in_=before[:, :], compare_op=ALU.is_gt, fill=0.0, base=0,
                                        pattern=[[1, P]], channel_multiplier=-1)

        consts = (ident, iota_e, iota_p, iota_c, before, ones_bf, tokp1, zeros)
        fw = (t["wexp"], t["shw"], t["wg"])
        ffn(nc, x, consts, fw, y_dram[0], xn_dram, ps, "f1")
        attention(nc, x, (t["wqkv"], t["wout"], t["wf"], t["bf"], t["bo"], (t["cos"], t["sin"]), t["four"]),
                  consts, ps)
        ffn(nc, x, consts, fw, y_dram[1], xn_dram, ps, "f2", out_dram=out)


def tables():
    pos = np.arange(SEQ, dtype=np.float32)[:, None]
    freqs = np.float32(10000.0) ** (-np.arange(0, DH, 2, dtype=np.float32) / np.float32(DH))
    ang = np.repeat(pos * freqs.astype(np.float32), 2, axis=1)
    sin, cos = np.sin(ang), np.cos(ang)
    sign = np.where(np.arange(DH) < DH // 2, -1.0, 1.0).astype(np.float32)
    pf = pos * np.arange(1, FREQS + 1, dtype=np.float32)
    four = np.concatenate([np.sin(pf), np.cos(pf)], axis=1).T

    def tile(a):
        return np.ascontiguousarray(a.reshape(TPB, P, DH).transpose(1, 0, 2)).astype(np.float32)
    return tile(cos), tile(sin * sign), np.ascontiguousarray(four).astype(np.float32)


def kernel(L0_attn_x, L0_attn_w_qkv, L0_attn_w_fproj, L0_attn_b_fproj, L0_attn_w_out, L0_attn_b_out, L0_ffn_wg,
           L0_ffn_shared_w1, L0_ffn_shared_w2, L0_ffn_expert_w1, L0_ffn_expert_w2):
    import concourse.bacc as bacc
    from concourse.bass_utils import run_bass_kernel_spmd

    def experts(w1, w2):
        a = np.asarray(w1).transpose(0, 2, 1)
        b = np.asarray(w2).transpose(0, 2, 1).reshape(-1, FC, P, DIM).transpose(0, 2, 1, 3).reshape(-1, P, FC * DIM)
        return np.ascontiguousarray(np.concatenate([a, b], axis=2))

    wqkv = np.asarray(L0_attn_w_qkv).reshape(3, PAIRS, P, DIM).transpose(3, 1, 0, 2).reshape(DIM, PAIRS, 3 * P)
    wout = np.asarray(L0_attn_w_out).T.reshape(PAIRS, P, DIM).transpose(1, 0, 2)
    wf = np.asarray(L0_attn_w_fproj).T
    bf = np.asarray(L0_attn_b_fproj).reshape(DH, 1)
    cos, sin, four = tables()
    arrays = {
        "x": np.asarray(L0_attn_x).reshape(TOKENS, DIM),
        "wexp": experts(L0_ffn_expert_w1, L0_ffn_expert_w2),
        "shw": experts(np.asarray(L0_ffn_shared_w1)[None], np.asarray(L0_ffn_shared_w2)[None])[0],
        "wg": np.asarray(L0_ffn_wg).T,
        "wqkv": wqkv, "wout": wout,
        "wf": np.concatenate([wf, wf], axis=1), "bf": np.concatenate([bf, bf], axis=0),
        "bo": np.broadcast_to(np.asarray(L0_attn_b_out), (P, DIM)),
        "cos": cos, "sin": sin, "four": four,
    }
    arrays = {n: np.ascontiguousarray(a) for n, a in arrays.items()}
    nc = bacc.Bacc("TRN2", target_bir_lowering=False, num_devices=1)
    t = {n: nc.dram_tensor(f"in_{n}", a.shape, mybir.dt.from_np(a.dtype), kind="ExternalInput").ap()
         for n, a in arrays.items()}
    out = nc.dram_tensor("out", [TOKENS, DIM], F32, kind="ExternalOutput").ap()
    build(nc, t, out)
    r = run_bass_kernel_spmd(nc, [{f"in_{n}": a for n, a in arrays.items()}], core_ids=[0])
    return r.results[0]["out"].reshape(BATCH, SEQ, DIM)
```

```python
from contextlib import ExitStack

import numpy as np

import concourse.bass as bass
from concourse import mybir

F32 = mybir.dt.float32
BF16 = mybir.dt.bfloat16
I32 = mybir.dt.int32
U32 = mybir.dt.uint32
ALU = mybir.AluOpType
ACT = mybir.ActivationFunctionType
AX = mybir.AxisListType

P = 128
BATCH, SEQ, DIM = 8, 256, 128
TOKENS = BATCH * SEQ
TILES = TOKENS // P
TPB = SEQ // P

HEADS, DH, FREQS = 16, 64, 16
INNER = HEADS * DH
PAIRS = HEADS // 2
SCALE = DH ** -0.5

EXPERTS, TOPK, FFN, CAPACITY = 64, 8, 384, 160
FC = FFN // P
WCOLS = 2 * FFN + FC * DIM
PLACES = EXPERTS * CAPACITY
COLS = PLACES // P
GE = 4
GT = GE * CAPACITY // P
GW = GE * CAPACITY
STEP_GROUPS = 2
STEP_EXPERTS = STEP_GROUPS * GE
STEPS = EXPERTS // STEP_EXPERTS
BLK = 512
BLOCKS = TOKENS // BLK
YROWS = TOKENS * TOPK
RANK_CAP = 240.0
FAR = 32768.0
EPS_LN = 1e-5
EPS_F32 = float(np.finfo(np.float32).eps)


def after(eng, sem, count):
    if not isinstance(count, int) or count > 0:
        eng.wait_ge(sem, count)


def ffn(nc, x, consts, w, ydram, xn_dram, ps, tag, out_dram=None):
    wexp, shw, wg = w
    ident, iota_e, iota_p, iota_c, before, ones_bf, tokp1, zeros = consts
    with ExitStack() as ctx:
        def sb(name, shape, dt=F32):
            return ctx.enter_context(nc.sbuf_tensor(f"{tag}_{name}", shape, dt))

        def sem(name):
            return ctx.enter_context(nc.semaphore(f"{tag}_{name}"))

        ring = sb("ring", [P, STEP_EXPERTS, WCOLS])
        take = sb("take", [P, COLS], I32)
        put = sb("put", [P, COLS], I32)
        wk = sb("wk", [P, TILES, TOPK])
        w_landed = [sem(f"w_landed{i}") for i in range(STEP_EXPERTS)]
        half_shared = sb("half_shared", [P, TILES, DIM])
        zeroed = sem("zeroed")
        xn_stored = sem("xn_stored")

        with ExitStack() as rctx:
            def rsb(name, shape, dt=F32):
                return rctx.enter_context(nc.sbuf_tensor(f"{tag}_{name}", shape, dt))

            def rsem(name):
                return rctx.enter_context(nc.semaphore(f"{tag}_{name}"))

            xn = rsb("xn", [P, TILES, DIM])
            xnT = rsb("xnT", [P, TOKENS])
            sq = half_shared
            st = rsb("st", [P, 4, TILES])
            pexp = rsb("pexp", [P, TILES])
            gate = rsb("gate", [P, TILES, EXPERTS])
            work = rsb("work", [P, TILES, EXPERTS])
            mask = rsb("mask", [P, TILES, EXPERTS], BF16)
            pre = rsb("pre", [P, 2, 8 + TILES, EXPERTS], BF16)
            top = rsb("top", [P, TILES, TOPK])
            topi = rsb("topi", [P, TILES, TOPK], U32)
            topf = rsb("topf", [P, TILES, TOPK])
            topr = rsb("topr", [P, TILES, TOPK, EXPERTS], BF16)
            hit = rsb("hit", [P, TILES, TOPK, EXPERTS], BF16)
            rankb = rsb("rankb", [P, TILES, EXPERTS], BF16)
            rk = rsb("rk", [P, TILES, TOPK])
            sm = rsb("sm", [P, 3, TILES])
            far = rsb("far", [P, TILES, TOPK])
            pl = rsb("pl", [P, TILES, TOPK])
            pli = rsb("pli", [P, TILES * TOPK], I32)
            lo_i = rsb("lo_i", [P, 2, TILES * TOPK], I32)
            lo = rsb("lo", [P, 2, TILES, TOPK], BF16)
            rowc = rsb("rowc", [P, TILES, TOPK], BF16)
            oh_p = rsb("oh_p", [P, 2, P, TOPK], BF16)
            oh_m = rsb("oh_m", [P, 2, COLS, TOPK], BF16)
            oh_c = rsb("oh_c", [P, 2, 2 * COLS, TOPK], BF16)
            tf = rsb("tf", [P, 6, COLS])
            ti = rsb("ti", [P, 4, COLS], I32)
            sil = rsb("sil", [P, 2, BLK])
            hid = rsb("hid", [P, 2, FC, BLK])
            shsb = rsb("shsb", [P, WCOLS])
            wgsb = rsb("wgsb", [P, EXPERTS])

            w_in = rsem("w_in")
            dv = rsem("dv")
            sqd = rsem("sqd")
            rstd = rsem("rstd")
            exped = rsem("exped")
            tps = rsem("tps")
            tsb = rsem("tsb")
            logit = rsem("logit")
            ranked = rsem("ranked")
            sh_h = rsem("sh_h")
            sh_c = rsem("sh_c")
            sh_a = rsem("sh_a")
            sh_o = rsem("sh_o")
            sh_x = rsem("sh_x")
            oh = rsem("oh")
            topr_in = rsem("topr_in")
            inv = rsem("inv")
            pconst = rsem("pconst")

            LOGB, RANKB, TRB, HB, OB, INVB = 0, 0, 2, 2, 6, 7
            OT = TILES // 2

            with nc.Block() as block:
                @block.sync
                def _(sp):
                    sp.dma_start(shsb[:, :], shw).then_inc(w_in, 16)
                    sp.dma_start(wgsb[:, :], wg).then_inc(w_in, 16)
                    for e in range(STEP_EXPERTS):
                        sp.dma_start(ring[:, e, :], wexp[e]).then_inc(w_landed[e], 16)
                    sp.wait_ge(dv, 6)
                    sp.dma_start(xn_dram.rearrange("(t p) d -> p t d", p=P), xn[:, :, :]).then_inc(xn_stored, 16)
                    y0 = ydram.rearrange("(c p r) d -> c p (r d)", p=P, r=TOPK)
                    for c in range(TILES):
                        sp.dma_start(y0[c], zeros[:, :]).then_inc(zeroed, 16)
                    sp.wait_ge(w_in, 32)

                @block.gpsimd
                def _(pool):
                    nc.gpsimd.memset(pexp[:, :], -0.5).then_inc(pconst, 1)
                    nc.gpsimd.memset(pre[:, :, 0:8, :], 0.0).then_inc(pconst, 1)
                    nc.gpsimd.iota(rowc[:, :, :].rearrange("p t k -> p (t k)"), [[1, TILES * TOPK]], base=0,
                                   channel_multiplier=0, allow_small_or_imprecise_dtypes=True).then_inc(pconst, 1)
                    pool.wait_ge(pconst, 1)
                    pool.wait_ge(dv, 5)
                    nc.gpsimd.tensor_tensor(st[:, 3, :], st[:, 2, :], pexp[:, :], ALU.pow).then_inc(rstd, 1)
                    for c in range(FC * BLOCKS):
                        b, f = c // FC, c % FC
                        pool.wait_ge(sh_c, c + 1)
                        nc.gpsimd.tensor_tensor(hid[:, b % 2, f, :], hid[:, b % 2, f, :], sil[:, c % 2, :],
                                                ALU.mult).then_inc(sh_a, 1)

                @block.vector
                def _(v):
                    n = [0]

                    def step(ins):
                        n[0] += 1
                        ins.then_inc(dv, 1)
                        v.wait_ge(dv, n[0])

                    def bc(ap, m):
                        return ap.unsqueeze(2).to_broadcast([P, TILES, m])

                    step(nc.vector.tensor_reduce(st[:, 0, :], x[:, :, :], AX.X, ALU.add))
                    step(nc.vector.tensor_scalar(st[:, 0, :], st[:, 0, :], 1.0 / DIM, None, ALU.mult))
                    step(nc.vector.tensor_tensor(xn[:, :, :], x[:, :, :], bc(st[:, 0, :], DIM), ALU.subtract))
                    v.wait_ge(sqd, 1)
                    step(nc.vector.tensor_reduce(st[:, 1, :], sq[:, :, :], AX.X, ALU.add))
                    step(nc.vector.tensor_scalar(st[:, 2, :], st[:, 1, :], 1.0 / DIM, EPS_LN, ALU.mult, ALU.add))
                    v.wait_ge(rstd, 1)
                    step(nc.vector.tensor_tensor(xn[:, :, :], xn[:, :, :], bc(st[:, 3, :], DIM), ALU.mult))
                    for c in range(BLOCKS):
                        v.wait_ge(tps, c + 1)
                        nc.vector.tensor_copy(xnT[:, c * BLK:(c + 1) * BLK], ps[:, TRB + c, :]).then_inc(tsb, 1)
                    v.wait_ge(logit, 1)
                    lg = ps[:, LOGB:LOGB + 2, :].rearrange("p b (t e) -> p (b t) e", e=EXPERTS)
                    step(nc.vector.tensor_reduce(sm[:, 0, :], lg, AX.X, ALU.max))
                    step(nc.vector.tensor_tensor(work[:, :, :], lg, bc(sm[:, 0, :], EXPERTS), ALU.subtract))
                    v.wait_ge(exped, 1)
                    step(nc.vector.tensor_reduce(sm[:, 1, :], gate[:, :, :], AX.X, ALU.add))
                    step(nc.vector.reciprocal(sm[:, 2, :], sm[:, 1, :]))
                    step(nc.vector.tensor_tensor(gate[:, :, :], gate[:, :, :], bc(sm[:, 2, :], EXPERTS), ALU.mult))
                    for t in range(TILES):
                        last = nc.vector.max(top[:, t, :], gate[:, t, :])
                    step(last)
                    for t in range(TILES):
                        last = nc.vector.max_index(topi[:, t, :], top[:, t, :], gate[:, t, :])
                    step(last)
                    step(nc.vector.tensor_copy(topf[:, :, :], topi[:, :, :]))
                    for t in range(TILES):
                        last = nc.vector.match_replace(work[:, t, :], top[:, t, :], gate[:, t, :], -1.0)
                    step(last)
                    step(nc.vector.tensor_scalar(pre[:, 0, 8:, :], work[:, :, :], 0.0, None, ALU.is_lt))
                    nc.vector.tensor_copy(mask[:, :, :], pre[:, 0, 8:, :])
                    v.wait_ge(pconst, 2)
                    for i, s in enumerate((1, 2, 4, 8)):
                        a, b = i % 2, (i + 1) % 2
                        step(nc.vector.tensor_tensor(pre[:, b, 8:, :], pre[:, a, 8:, :],
                                                     pre[:, a, 8 - s:8 - s + TILES, :], ALU.add))
                    step(nc.vector.tensor_reduce(sm[:, 0, :], top[:, :, :], AX.X, ALU.add))
                    step(nc.vector.tensor_scalar(sm[:, 0, :], sm[:, 0, :], EPS_F32, None, ALU.max))
                    step(nc.vector.reciprocal(sm[:, 1, :], sm[:, 0, :]))
                    step(nc.vector.scalar_tensor_tensor(wk[:, :, :], top[:, :, :], 0.5, bc(sm[:, 1, :], TOPK),
                                                        ALU.mult, ALU.mult))
                    v.wait_ge(topr_in, 1)
                    step(nc.vector.tensor_tensor(
                        hit[:, :, :, :].rearrange("p t k e -> p (t k) e"), topr[:, :, :, :].rearrange("p t k e -> p (t k) e"),
                        iota_e[:, :].unsqueeze(1).to_broadcast([P, TILES * TOPK, EXPERTS]), ALU.is_equal))
                    v.wait_ge(ranked, 1)
                    step(nc.vector.tensor_scalar(rankb[:, :, :].rearrange("p t e -> p (t e)"),
                                                 ps[:, RANKB:RANKB + 2, :].rearrange("p b c -> p (b c)"),
                                                 RANK_CAP, None, ALU.min))
                    step(nc.vector.tensor_tensor(hit[:, :, :, :], hit[:, :, :, :],
                                                 rankb[:, :, :].unsqueeze(2).to_broadcast([P, TILES, TOPK, EXPERTS]),
                                                 ALU.mult))
                    hv = hit[:, :, :, :].rearrange("p t k e -> p (t k) e")
                    half = EXPERTS // 2
                    while half >= 2:
                        step(nc.vector.tensor_tensor(hv[:, :, 0:half], hv[:, :, 0:half], hv[:, :, half:2 * half],
                                                     ALU.add))
                        half //= 2
                    step(nc.vector.tensor_tensor(rk[:, :, :].rearrange("p t k -> p (t k)"), hv[:, :, 0], hv[:, :, 1],
                                                 ALU.add))
                    step(nc.vector.tensor_scalar(far[:, :, :], rk[:, :, :], CAPACITY - 0.5, FAR, ALU.is_gt, ALU.mult))
                    step(nc.vector.scalar_tensor_tensor(pl[:, :, :], topf[:, :, :], float(CAPACITY), rk[:, :, :],
                                                        ALU.mult, ALU.add))
                    step(nc.vector.tensor_tensor(pli[:, :], pl[:, :, :].rearrange("p t k -> p (t k)"),
                                                 far[:, :, :].rearrange("p t k -> p (t k)"), ALU.add))
                    nc.vector.tensor_scalar(lo_i[:, 0, :], pli[:, :], P - 1, None, ALU.bitwise_and)
                    step(nc.vector.tensor_scalar(lo_i[:, 1, :], pli[:, :], 7, None, ALU.logical_shift_right))
                    step(nc.vector.tensor_copy(lo[:, :, :, :].rearrange("p a t k -> p a (t k)"), lo_i[:, :, :]))
                    v.wait_ge(pconst, 3)
                    base = n[0]
                    with v.Fori(0, OT) as i:
                        for h in range(2):
                            t = 2 * i + h
                            v.wait_ge(inv, t + 1)
                            lo_t = lo[:, :, bass.ds(t, 1), :]

                            def bk(ap, m):
                                return ap.to_broadcast([P, m, TOPK])
                            nc.vector.tensor_tensor(oh_p[:, h, :, :], iota_p[:, :, :], bk(lo_t[:, 0, :, :], P),
                                                    ALU.is_equal)
                            nc.vector.tensor_tensor(oh_m[:, h, :, :], iota_c[:, :, :], bk(lo_t[:, 1, :, :], COLS),
                                                    ALU.is_equal).then_inc(dv, 1)
                            v.wait_ge(dv, base + t + 1)
                            nc.vector.tensor_tensor(oh_c[:, h, 0:COLS, :], oh_m[:, h, :, :],
                                                    tokp1[:, :].unsqueeze(1).to_broadcast([P, COLS, TOPK]), ALU.mult)
                            nc.vector.tensor_tensor(oh_c[:, h, COLS:, :], oh_m[:, h, :, :],
                                                    bk(rowc[:, bass.ds(t, 1), :], COLS), ALU.mult).then_inc(oh, 1)
                    n[0] = base + TILES
                    v.wait_ge(inv, TILES + 2)
                    step(nc.vector.tensor_copy(tf[:, 0:2, :].rearrange("p a c -> p (a c)"), ps[:, INVB, 0:2 * COLS]))
                    step(nc.vector.tensor_copy(ti[:, 0, :], tf[:, 1, :]))
                    nc.vector.tensor_scalar(ti[:, 1, :], ti[:, 0, :], 3, None, ALU.logical_shift_right)
                    step(nc.vector.tensor_scalar(ti[:, 2, :], ti[:, 0, :], TOPK - 1, None, ALU.bitwise_and))
                    step(nc.vector.tensor_copy(tf[:, 2:4, :], ti[:, 1:3, :]))
                    step(nc.vector.scalar_tensor_tensor(tf[:, 4, :], tf[:, 2, :], float(P), tf[:, 0, :],
                                                        ALU.mult, ALU.add))
                    step(nc.vector.tensor_scalar(tf[:, 4, :], tf[:, 4, :], -1.0, None, ALU.add))
                    nc.vector.tensor_scalar(take[:, :], tf[:, 4, :], 0.0, None, ALU.max)
                    step(nc.vector.scalar_tensor_tensor(tf[:, 5, :], tf[:, 4, :], float(TOPK), tf[:, 3, :],
                                                        ALU.mult, ALU.add))
                    step(nc.vector.tensor_scalar(tf[:, 4, :], tf[:, 0, :], 0.5, FAR, ALU.is_lt, ALU.mult))
                    step(nc.vector.tensor_tensor(put[:, :], tf[:, 5, :], tf[:, 4, :], ALU.add))

                SUMMED = 20

                @block.tensor
                def _(pe):
                    nc.tensor.matmul(ps[:, INVB, 0:2 * COLS], zeros[:, 0:P // 2].bitcast(BF16),
                                     zeros[:, 0:COLS].bitcast(BF16), start=True, stop=True).then_inc(inv, 2)
                    pe.wait_ge(dv, 6)
                    for t in range(TILES):
                        mm = nc.tensor.transpose(ps[:, TRB + t // 4, (t % 4) * P:(t % 4 + 1) * P], xn[:, t, :],
                                                 ident[:, :])
                        if t % 4 == 3:
                            mm.then_inc(tps, 1)
                    pe.wait_ge(w_in, 32)
                    for t in range(TILES):
                        if t % 4 == 0:
                            pe.wait_ge(tsb, t // 4 + 1)
                        mm = nc.tensor.matmul(ps[:, LOGB + t // 8, (t % 8) * EXPERTS:(t % 8 + 1) * EXPERTS],
                                              xnT[:, t * P:(t + 1) * P], wgsb[:, :], start=True, stop=True)
                    mm.then_inc(logit, 1)

                    def up(c):
                        b, f, h = c // FC, c % FC, c % 2
                        if c == 0:
                            pe.wait_ge(tsb, BLOCKS)
                        if c >= 2:
                            pe.wait_ge(sh_c, c - 1)
                        for half in range(2):
                            mm = nc.tensor.matmul(ps[:, HB + 2 * h + half, :],
                                                  shsb[:, half * FFN + f * P:half * FFN + (f + 1) * P],
                                                  xnT[:, b * BLK:(b + 1) * BLK], start=True, stop=True)
                        mm.then_inc(sh_h, 1)

                    def down(b):
                        pe.wait_ge(sh_a, FC * (b + 1))
                        if b >= 1:
                            pe.wait_ge(sh_x, b)
                        for j in range(BLK // P):
                            for f in range(FC):
                                mm = nc.tensor.matmul(ps[:, OB, j * P:(j + 1) * P],
                                                      hid[:, b % 2, f, j * P:(j + 1) * P],
                                                      shsb[:, 2 * FFN + f * DIM:2 * FFN + (f + 1) * DIM],
                                                      start=(f == 0), stop=(f == FC - 1))
                        mm.then_inc(sh_o, 1)

                    def ranks():
                        pe.wait_ge(dv, SUMMED)
                        for t in range(TILES):
                            o = ps[:, RANKB + t // 8, (t % 8) * EXPERTS:(t % 8 + 1) * EXPERTS]
                            mm = nc.tensor.matmul(o, before[:, :], mask[:, t, :], start=True, stop=(t == 0))
                            if t:
                                mm = nc.tensor.matmul(o, ones_bf[:, :], pre[:, 0, 8 + t - 1, :],
                                                      start=False, stop=True)
                        mm.then_inc(ranked, 1)

                    for c in range(FC * BLOCKS):
                        up(c)
                        if c == 7:
                            ranks()
                        if c % FC == 0 and c:
                            down(c // FC - 1)
                    down(BLOCKS - 1)
                    with pe.Fori(0, OT) as i:
                        for h in range(2):
                            pe.wait_ge(oh, 2 * i + h + 1)
                            for k in range(TOPK):
                                mm = nc.tensor.matmul(ps[:, INVB, 0:2 * COLS], oh_p[:, h, :, k], oh_c[:, h, :, k],
                                                      start=False, stop=False, skip_group_check=True)
                            mm.then_inc(inv, 1)

                @block.scalar
                def _(act):
                    act.wait_ge(dv, 3)
                    nc.scalar.activation(sq[:, :, :], xn[:, :, :], ACT.Square).then_inc(sqd, 1)
                    act.wait_ge(dv, 8)
                    nc.scalar.activation(gate[:, :, :], work[:, :, :], ACT.Exp).then_inc(exped, 1)

                    act.wait_ge(dv, 14)
                    nc.scalar.copy(topr[:, :, :, :].rearrange("p t k e -> p (t k) e"),
                                   topf[:, :, :].rearrange("p t k -> p (t k)").unsqueeze(2).to_broadcast(
                                       [P, TILES * TOPK, EXPERTS])).then_inc(topr_in, 1)

                    def half_down(b):
                        act.wait_ge(sh_o, b + 1)
                        nc.scalar.mul(sq[:, b * 4:(b + 1) * 4, :].rearrange("p t d -> p (t d)"), ps[:, OB, :],
                                      0.5).then_inc(sh_x, 1)

                    act.wait_ge(dv, 4)
                    for c in range(FC * BLOCKS):
                        b, f = c // FC, c % FC
                        act.wait_ge(sh_h, c + 1)
                        if c >= 2:
                            act.wait_ge(sh_a, c - 1)
                        nc.scalar.activation(sil[:, c % 2, :], ps[:, HB + 2 * (c % 2) + 1, :], ACT.Silu)
                        if b >= 2:
                            act.wait_ge(sh_o, b - 1)
                        nc.scalar.copy(hid[:, b % 2, f, :], ps[:, HB + 2 * (c % 2), :]).then_inc(sh_c, 1)
                        if c % FC == FC - 1 and b >= 1:
                            half_down(b - 1)
                    half_down(BLOCKS - 1)

        with ExitStack() as ectx:
            def esb(name, shape, dt=F32):
                return ectx.enter_context(nc.sbuf_tensor(f"{tag}_{name}", shape, dt))

            def esem(name):
                return ectx.enter_context(nc.semaphore(f"{tag}_{name}"))

            SG = STEP_GROUPS
            tk = esb("tk", [P, SG, GT], I32)
            pt = esb("pt", [P, SG, GT], I32)
            xg = esb("xg", [P, SG, GT, DIM])
            xgT = esb("xgT", [P, SG, GW])
            sil = esb("esil", [P, 2, FC * CAPACITY])
            hid = esb("ehid", [P, 2, FC * CAPACITY])
            oT = esb("oT", [P, SG, GW])
            og = esb("og", [P, SG, GT, DIM])

            passed = esem("passed")
            tk_in = esem("tk_in")
            pt_in = esem("pt_in")
            got = [esem(f"got{g}") for g in range(SG)]
            sent = [esem(f"sent{g}") for g in range(SG)]
            xg_t = esem("xg_t")
            xg_s = esem("xg_s")
            hb = esem("hb")
            sl = esem("sl")
            ac = esem("ac")
            ob = esem("ob")
            os_ = esem("os")
            og_t = esem("og_t")
            og_s = esem("og_s")
            XB, HB, OB, GB = 0, 2, 6, 7

            with nc.Block() as block:
                @block.sync
                def _(sp):
                    with sp.Fori(1, STEPS) as i:
                        for e in range(STEP_EXPERTS):
                            sp.wait_ge(ob, STEP_EXPERTS * (i - 1) + e + 1)
                            sp.dma_start(ring[:, e, :], wexp[bass.ds(STEP_EXPERTS * i + e, 1), :, :].rearrange(
                                "e p c -> (e p) c")).then_inc(w_landed[e], 16)

                @block.gpsimd
                def _(pool):
                    def gather(i, g):
                        G = SG * i + g
                        after(pool, xg_t, G - 1)
                        pool.wait_ge(xn_stored, 16)
                        nc.gpsimd.tensor_copy(tk[:, g, :], take[:, bass.ds(G * GT, GT)]).then_inc(tk_in, 1)
                        pool.wait_ge(tk_in, G + 1)
                        pool.sem_inc(passed, 1)
                        for s in range(GT):
                            nc.gpsimd.indirect_dma_start(
                                xg[:, g, s, :], None, xn_dram, bass.IndirectOffsetOnAxis(tk[:, g, s:s + 1], 0),
                                bounds_check=TOKENS - 1, oob_is_err=False).then_inc(got[g], 16)

                    def scatter(i, g):
                        G = SG * i + g
                        after(pool, sent[g], 16 * GT * i)
                        pool.wait_ge(zeroed, 16 * TILES)
                        nc.gpsimd.tensor_copy(pt[:, g, :], put[:, bass.ds(G * GT, GT)]).then_inc(pt_in, 1)
                        pool.wait_ge(pt_in, G + 1)
                        pool.wait_ge(og_s, 2 * G + 2)
                        pool.sem_inc(passed, 1)
                        for s in range(GT):
                            nc.gpsimd.indirect_dma_start(
                                ydram, bass.IndirectOffsetOnAxis(pt[:, g, s:s + 1], 0), og[:, g, s, :], None,
                                bounds_check=YROWS - 1, oob_is_err=False).then_inc(sent[g], 16)

                    for g in range(SG):
                        gather(0, g)
                    for g in range(SG):
                        gather(1, g)
                    for g in range(SG):
                        scatter(0, g)
                        gather(2, g)
                    with pool.Fori(3, STEPS) as i:
                        for g in range(SG):
                            scatter(i - 2, g)
                            gather(i, g)
                    for i in (STEPS - 2, STEPS - 1):
                        for g in range(SG):
                            scatter(i, g)
                    for g in range(SG):
                        pool.wait_ge(sent[g], 16 * GT * STEPS)

                @block.tensor
                def _(pe):
                    def turn_in(i, g):
                        G = SG * i + g
                        after(pe, xg_s, G)
                        pe.wait_ge(got[g], 16 * GT * i + 16 * GT)
                        for s in range(GT):
                            mm = nc.tensor.transpose(ps[:, XB + s // 4, (s % 4) * P:(s % 4 + 1) * P],
                                                     xg[:, g, s, :], ident[:, :])
                        mm.then_inc(xg_t, 1)

                    def up(i, e):
                        g, E = e // GE, STEP_EXPERTS * i + e
                        pe.wait_ge(w_landed[e], 16 * i + 16)
                        if e % GE == 0:
                            pe.wait_ge(xg_s, SG * i + g + 1)
                        after(pe, ac, E - 1)
                        a = (e % GE) * CAPACITY
                        for half in range(2):
                            for f in range(FC):
                                mm = nc.tensor.matmul(
                                    ps[:, HB + 2 * (e % 2) + half, f * CAPACITY:(f + 1) * CAPACITY],
                                    ring[:, e, half * FFN + f * P:half * FFN + (f + 1) * P],
                                    xgT[:, g, a:a + CAPACITY], start=True, stop=True)
                        mm.then_inc(hb, 1)

                    def down(i, e):
                        E = STEP_EXPERTS * i + e
                        pe.wait_ge(ac, E + 1)
                        after(pe, os_, E)
                        for f in range(FC):
                            mm = nc.tensor.matmul(ps[:, OB, 0:CAPACITY],
                                                  ring[:, e, 2 * FFN + f * DIM:2 * FFN + (f + 1) * DIM],
                                                  hid[:, e % 2, f * CAPACITY:(f + 1) * CAPACITY],
                                                  start=(f == 0), stop=(f == FC - 1))
                        mm.then_inc(ob, 1)

                    def turn_out(i, g, part):
                        G = SG * i + g
                        pe.wait_ge(os_, GE * (G + 1))
                        after(pe, og_s, 2 * G + part)
                        for s in range(3) if part == 0 else range(3, GT):
                            mm = nc.tensor.transpose(ps[:, GB, (s % 3) * P:(s % 3 + 1) * P],
                                                     oT[:, g, s * P:(s + 1) * P], ident[:, :])
                        mm.then_inc(og_t, 1)

                    def step(i, first, last):
                        for e in range(STEP_EXPERTS):
                            g, r = e // GE, e % GE
                            if r == 2 and not (last and g == SG - 1):
                                turn_in(*((i, g + 1) if g < SG - 1 else (i + 1, 0)))
                            if e < STEP_EXPERTS - 1:
                                up(i, e + 1)
                            elif not last:
                                up(i + 1, 0)
                            down(i, e)
                            if r in (0, 1) and not (first and g == 0):
                                turn_out(*((i, g - 1) if g else (i - 1, SG - 1)), r)

                    turn_in(0, 0)
                    up(0, 0)
                    step(0, True, False)
                    step(1, False, False)
                    with pe.Fori(2, STEPS - 1) as i:
                        step(i, False, False)
                    step(STEPS - 1, False, True)
                    turn_out(STEPS - 1, SG - 1, 0)
                    turn_out(STEPS - 1, SG - 1, 1)

                @block.scalar
                def _(act):
                    def group_in(i, g):
                        G = SG * i + g
                        act.wait_ge(xg_t, G + 1)
                        after(act, hb, GE * (G - 1))
                        nc.scalar.copy(xgT[:, g, :], ps[:, XB:XB + 2, :].rearrange("p b c -> p (b c)")[:, 0:GW]
                                       ).then_inc(xg_s, 1)

                    def silu(i, e):
                        E = STEP_EXPERTS * i + e
                        act.wait_ge(hb, E + 1)
                        after(act, ac, E - 1)
                        nc.scalar.activation(sil[:, e % 2, :], ps[:, HB + 2 * (e % 2) + 1, 0:FC * CAPACITY],
                                             ACT.Silu).then_inc(sl, 1)

                    def group_out(i, g, part):
                        G = SG * i + g
                        act.wait_ge(og_t, 2 * G + part + 1)
                        if part == 0:
                            after(act, sent[g], 16 * GT * i)
                        a, b = ((0, 3), (3, GT))[part]
                        nc.scalar.copy(og[:, g, a:b, :].rearrange("p s d -> p (s d)"),
                                       ps[:, GB, 0:(b - a) * P]).then_inc(og_s, 1)

                    def step(i, first, last):
                        for e in range(STEP_EXPERTS):
                            g, r = e // GE, e % GE
                            if r == 2 and not (last and g == SG - 1):
                                group_in(*((i, g + 1) if g < SG - 1 else (i + 1, 0)))
                            if e < STEP_EXPERTS - 1:
                                silu(i, e + 1)
                            elif not last:
                                silu(i + 1, 0)
                            if r in (0, 1) and not (first and g == 0):
                                group_out(*((i, g - 1) if g else (i - 1, SG - 1)), r)

                    group_in(0, 0)
                    silu(0, 0)
                    step(0, True, False)
                    step(1, False, False)
                    with act.Fori(2, STEPS - 1) as i:
                        step(i, False, False)
                    step(STEPS - 1, False, True)
                    group_out(STEPS - 1, SG - 1, 0)
                    group_out(STEPS - 1, SG - 1, 1)

                @block.vector
                def _(v):
                    nc.vector.tensor_tensor(x[:, :, :], x[:, :, :], half_shared[:, :, :], ALU.add)

                    def product(i, e):
                        E = STEP_EXPERTS * i + e
                        v.wait_ge(sl, E + 1)
                        after(v, ob, E - 1)
                        nc.vector.tensor_tensor(hid[:, e % 2, :], sil[:, e % 2, :],
                                                ps[:, HB + 2 * (e % 2), 0:FC * CAPACITY], ALU.mult).then_inc(ac, 1)

                    def output(i, e):
                        g, E = e // GE, STEP_EXPERTS * i + e
                        v.wait_ge(ob, E + 1)
                        if e % GE == 0:
                            after(v, og_t, 2 * (SG * i + g - 1))
                        a = (e % GE) * CAPACITY
                        nc.vector.tensor_copy(oT[:, g, a:a + CAPACITY], ps[:, OB, 0:CAPACITY]).then_inc(os_, 1)

                    def step(i, first, last):
                        for e in range(STEP_EXPERTS):
                            if e < STEP_EXPERTS - 1:
                                product(i, e + 1)
                            elif not last:
                                product(i + 1, 0)
                            output(i, e)

                    product(0, 0)
                    step(0, True, False)
                    step(1, False, False)
                    with v.Fori(2, STEPS - 1) as i:
                        step(i, False, False)
                    step(STEPS - 1, False, True)

        with ExitStack() as cctx:
            YB = 4
            yt = cctx.enter_context(nc.sbuf_tensor(f"{tag}_yt", [P, 2, YB, TOPK * DIM], F32))
            y_in = [cctx.enter_context(nc.semaphore(f"{tag}_y_in{q}")) for q in range(2)]
            summed = cctx.enter_context(nc.semaphore(f"{tag}_summed"))
            stored = cctx.enter_context(nc.semaphore(f"{tag}_stored"))
            ysrc = ydram.rearrange("(c p r) d -> c p (r d)", p=P, r=TOPK)
            QS = TILES // YB
            with nc.Block() as block:
                @block.sync
                def _(sp):
                    for q in range(QS):
                        if q >= 2:
                            sp.wait_ge(summed, TOPK * (q - 1))
                        sp.dma_start(yt[:, q % 2, :, :], ysrc[q * YB:(q + 1) * YB].rearrange("c p w -> p c w")
                                     ).then_inc(y_in[q % 2], 16)
                    if out_dram is not None:
                        dst = out_dram.rearrange("(t p) d -> p t d", p=P)
                        for q in range(QS):
                            sp.wait_ge(summed, TOPK * (q + 1))
                            sp.dma_start(dst[:, q * YB:(q + 1) * YB, :], x[:, q * YB:(q + 1) * YB, :]
                                         ).then_inc(stored, 16)
                        sp.wait_ge(stored, 16 * QS)

                @block.vector
                def _(v):
                    n = 0
                    for q in range(QS):
                        v.wait_ge(y_in[q % 2], 16 * (q // 2 + 1))
                        for k in range(TOPK):
                            if k:
                                v.wait_ge(summed, n)
                            for j in range(YB):
                                t = q * YB + j
                                last = nc.vector.scalar_tensor_tensor(
                                    x[:, t, :], yt[:, q % 2, j, k * DIM:(k + 1) * DIM], wk[:, t, k:k + 1],
                                    x[:, t, :], ALU.mult, ALU.add)
                            n += 1
                            last.then_inc(summed, 1)



def attention(nc, x, attn_w, consts, ps):
    wqkv, wout, wf, bf, bo, tabs, four = attn_w
    ident = consts[0]
    with ExitStack() as ctx:
        def sb(name, shape, dt=F32):
            return ctx.enter_context(nc.sbuf_tensor(f"at_{name}", shape, dt))

        def sem(name):
            return ctx.enter_context(nc.semaphore(f"at_{name}"))

        QKW = 2 * P
        wq_sb = sb("wqkv", [P, PAIRS, 3 * P])
        wo_sb = sb("wout", [P, PAIRS, DIM])
        wf_sb = sb("wf", [2 * FREQS, QKW])
        four_sb = sb("four", [2 * FREQS, SEQ])
        bf_sb = sb("bf", [P, QKW])
        bo_sb = sb("bo", [P, DIM])
        cos = sb("cos", [P, TPB, QKW])
        sin = sb("sin", [P, TPB, QKW])
        fenc = sb("fenc", [P, TPB, QKW])
        xall = sb("xall", [P, TOKENS])
        xcur = sb("xcur", [P, SEQ])
        xnext = sb("xnext", [P, SEQ])

        loaded = sem("loaded")
        ready = sem("ready")
        with ExitStack() as lctx:
            xn = lctx.enter_context(nc.sbuf_tensor("at_xn", [P, TILES, DIM], F32))
            sq = lctx.enter_context(nc.sbuf_tensor("at_sq", [P, TILES, DIM], F32))
            st = lctx.enter_context(nc.sbuf_tensor("at_st", [P, 4, TILES], F32))
            pexp = lctx.enter_context(nc.sbuf_tensor("at_pexp", [P, TILES], F32))
            dv, sqd, rstd, tps, fe = (lctx.enter_context(nc.semaphore(f"at_{q}"))
                                      for q in ("dv", "sqd", "rstd", "tps", "fe"))
            with nc.Block() as block:
                @block.sync
                def _(sp):
                    for dst, src in ((wq_sb[:, :, :], wqkv), (wo_sb[:, :, :], wout), (wf_sb[:, :], wf),
                                     (four_sb[:, :], four), (bf_sb[:, :], bf), (bo_sb[:, :], bo),
                                     (cos[:, :, :], tabs[0]), (sin[:, :, :], tabs[1])):
                        sp.dma_start(dst, src).then_inc(loaded, 16)
                    sp.wait_ge(loaded, 128)

                @block.gpsimd
                def _(pool):
                    nc.gpsimd.memset(pexp[:, :], -0.5).then_inc(ready, 1)
                    pool.wait_ge(ready, 1)
                    pool.wait_ge(dv, 5)
                    nc.gpsimd.tensor_tensor(st[:, 3, :], st[:, 2, :], pexp[:, :], ALU.pow).then_inc(rstd, 1)

                @block.vector
                def _(v):
                    n = [0]

                    def step(ins):
                        n[0] += 1
                        ins.then_inc(dv, 1)
                        v.wait_ge(dv, n[0])

                    def bc(ap):
                        return ap.unsqueeze(2).to_broadcast([P, TILES, DIM])

                    step(nc.vector.tensor_reduce(st[:, 0, :], x[:, :, :], AX.X, ALU.add))
                    step(nc.vector.tensor_scalar(st[:, 0, :], st[:, 0, :], 1.0 / DIM, None, ALU.mult))
                    step(nc.vector.tensor_tensor(xn[:, :, :], x[:, :, :], bc(st[:, 0, :]), ALU.subtract))
                    v.wait_ge(sqd, 1)
                    step(nc.vector.tensor_reduce(st[:, 1, :], sq[:, :, :], AX.X, ALU.add))
                    step(nc.vector.tensor_scalar(st[:, 2, :], st[:, 1, :], 1.0 / DIM, EPS_LN, ALU.mult, ALU.add))
                    v.wait_ge(rstd, 1)
                    step(nc.vector.tensor_tensor(xn[:, :, :], xn[:, :, :], bc(st[:, 3, :]), ALU.mult))
                    v.wait_ge(loaded, 128)
                    nc.vector.tensor_tensor(x[:, :, :], x[:, :, :],
                                            bo_sb[:, :].unsqueeze(1).to_broadcast([P, TILES, DIM]), ALU.add)
                    v.wait_ge(fe, 1)
                    step(nc.vector.tensor_tensor(fenc[:, :, :], ps[:, 0, :].rearrange("p (t c) -> p t c", t=TPB),
                                                 bf_sb[:, :].unsqueeze(1).to_broadcast([P, TPB, QKW]), ALU.add))
                    step(nc.vector.tensor_scalar(fenc[:, :, 0:P], fenc[:, :, 0:P], SCALE, None, ALU.mult))
                    for c in range(BLOCKS):
                        v.wait_ge(tps, c + 1)
                        nc.vector.tensor_copy(xall[:, c * BLK:(c + 1) * BLK], ps[:, 2 + c, :])

                @block.scalar
                def _(act):
                    act.wait_ge(dv, 3)
                    nc.scalar.activation(sq[:, :, :], xn[:, :, :], ACT.Square).then_inc(sqd, 1)

                @block.tensor
                def _(pe):
                    pe.wait_ge(loaded, 128)
                    for t in range(TPB):
                        mm = nc.tensor.matmul(ps[:, 0, t * QKW:(t + 1) * QKW], four_sb[:, t * P:(t + 1) * P],
                                              wf_sb[:, :], start=True, stop=True)
                    mm.then_inc(fe, 1)
                    pe.wait_ge(dv, 6)
                    for t in range(TILES):
                        mm = nc.tensor.transpose(ps[:, 2 + t // 4, (t % 4) * P:(t % 4 + 1) * P], xn[:, t, :],
                                                 ident[:, :])
                        if t % 4 == 3:
                            mm.then_inc(tps, 1)

        m1 = sb("m1", [P, 2, TPB * QKW])
        m2 = sb("m2", [P, 2, TPB * QKW])
        vsb = sb("v", [P, PAIRS, TPB, P])
        qT = sb("qT", [P, 2, SEQ])
        kT = sb("kT", [P, 2, 2, SEQ])
        nmax = sb("nmax", [P, 2, 2, TPB])
        rsum = sb("rsum", [P, 2, 2, TPB])
        rinv = sb("rinv", [P, 2, 2, TPB])
        prob = sb("prob", [P, 2, 2, TPB, SEQ])
        pT = sb("pT", [P, 2, TPB, SEQ])
        oT = sb("oTh", [P, PAIRS, SEQ])

        passed = sem("passed")
        xc, xx = sem("xc"), sem("xx")
        qk, vp = sem("qk"), sem("vp")
        rope, fadd, msum = sem("rope"), sem("fadd"), sem("msum")
        vev, tq = sem("vev"), sem("tq")
        qkev = sem("qkev")
        sc, mx, ex = sem("sc"), sem("mx"), sem("ex")
        rc, pn = sem("rc"), sem("pn")
        pt, pte = sem("pt"), sem("pte")
        pv, oev = sem("pv"), sem("oev")
        op, res, z = sem("op"), sem("res"), sem("z")
        QB, VB, TB, SB, PB, OB = 0, 1, 2, 3, 5, 7
        AHEAD = 3

        def pair(b, p, ahead):
            return (b, p + ahead) if p + ahead < PAIRS else (b + 1, p + ahead - PAIRS)

        def earlier(b, p, back):
            return (b, p - back) if p >= back else (b - 1, p - back + PAIRS)

        def there(b, p, back, first, last):
            return not (first and p - back < 0) and not (last and p - back >= PAIRS)

        with nc.Block() as block:
            @block.gpsimd
            def _(pool):
                nc.gpsimd.memset(kT[:, :, :, :], 0.0).then_inc(z, 1)

                def load_cur(b):
                    after(pool, vp, PAIRS * b)
                    pool.sem_inc(passed, 1)
                    nc.gpsimd.tensor_copy(xcur[:, :], xall[:, bass.ds(b * SEQ, SEQ)]).then_inc(xc, 1)

                def load_next(b):
                    after(pool, vp, PAIRS * (b - 1) + AHEAD)
                    pool.sem_inc(passed, 1)
                    nc.gpsimd.tensor_copy(xnext[:, :], xall[:, bass.ds(b * SEQ, SEQ)]).then_inc(xx, 1)

                def add(b, p):
                    u = PAIRS * b + p
                    pool.wait_ge(rope, u + 1)
                    nc.gpsimd.tensor_tensor(m1[:, p % 2, :], m1[:, p % 2, :], m2[:, p % 2, :],
                                            ALU.add).then_inc(fadd, 1)
                    pool.wait_ge(fadd, u + 1)
                    nc.gpsimd.tensor_tensor(m1[:, p % 2, :], m1[:, p % 2, :],
                                            fenc[:, :, :].rearrange("p t c -> p (t c)"), ALU.add).then_inc(msum, 1)

                def batch(b, last):
                    for p in range(PAIRS):
                        if there(b, p, -2, False, last):
                            add(*pair(b, p, 2))
                        if p == 0 and not last:
                            load_next(b + 1)
                        if p == PAIRS - AHEAD and not last:
                            load_cur(b + 1)

                load_cur(0)
                add(0, 0)
                add(0, 1)
                batch(0, False)
                with pool.Fori(1, BATCH - 1) as b:
                    batch(b, False)
                batch(BATCH - 1, True)

            @block.tensor
            def _(pe):
                def qkv(b, p, xs):
                    u = PAIRS * b + p
                    after(pe, rope, u)
                    for t in range(TPB):
                        mm = nc.tensor.matmul(ps[:, QB, t * QKW:(t + 1) * QKW], xs[:, t * P:(t + 1) * P],
                                              wq_sb[:, p, 0:QKW], start=True, stop=True)
                    mm.then_inc(qk, 1)
                    after(pe, vev, u)
                    for t in range(TPB):
                        mm = nc.tensor.matmul(ps[:, VB, t * P:(t + 1) * P], xs[:, t * P:(t + 1) * P],
                                              wq_sb[:, p, QKW:], start=True, stop=True)
                    mm.then_inc(vp, 1)

                def turn(b, p):
                    u = PAIRS * b + p
                    pe.wait_ge(msum, u + 1)
                    after(pe, qkev, u)
                    for half in range(2):
                        for t in range(TPB):
                            mm = nc.tensor.transpose(ps[:, TB, half * SEQ + t * P:half * SEQ + (t + 1) * P],
                                                     m1[:, p % 2, t * QKW + half * P:t * QKW + (half + 1) * P],
                                                     ident[:, :])
                    mm.then_inc(tq, 1)

                def scores(b, p, h):
                    u = PAIRS * b + p
                    if h == 0:
                        pe.wait_ge(qkev, u + 1)
                    after(pe, ex, 2 * u + h - 1)
                    for t in range(TPB):
                        mm = nc.tensor.matmul(ps[:, SB + h, t * SEQ:(t + 1) * SEQ], qT[:, p % 2, t * P:(t + 1) * P],
                                              kT[:, p % 2, h, :], start=True, stop=True)
                    mm.then_inc(sc, 1)

                def turn_p(b, p, h):
                    u = PAIRS * b + p
                    pe.wait_ge(pn, 2 * u + h + 1)
                    after(pe, pte, 2 * u + h - 1)
                    for t in range(TPB):
                        for j in range(TPB):
                            mm = nc.tensor.transpose(ps[:, PB + h, j * SEQ + t * P:j * SEQ + (t + 1) * P],
                                                     prob[:, p % 2, h, t, j * P:(j + 1) * P], ident[:, :])
                    mm.then_inc(pt, 1)

                def values(b, p):
                    u = PAIRS * b + p
                    pe.wait_ge(vev, u + 1)
                    after(pe, oev, u)
                    for h in range(2):
                        pe.wait_ge(pte, 2 * u + h + 1)
                        for j in range(TPB):
                            mm = nc.tensor.matmul(ps[h * DH:(h + 1) * DH, OB, 0:SEQ],
                                                  vsb[:, p, j, h * DH:(h + 1) * DH], pT[:, h, j, :],
                                                  start=(j == 0), stop=(j == TPB - 1))
                        mm.then_inc(pv, 1)

                def project(b):
                    pe.wait_ge(oev, PAIRS * (b + 1))
                    for t in range(TPB):
                        for p in range(PAIRS):
                            mm = nc.tensor.matmul(ps[:, OB, t * DIM:(t + 1) * DIM],
                                                  oT[:, p, t * P:(t + 1) * P], wo_sb[:, p, :],
                                                  start=(p == 0), stop=(p == PAIRS - 1))
                    mm.then_inc(op, 1)

                def batch(b, first, last):
                    for p in range(PAIRS):
                        scores(b, p, 0)
                        scores(b, p, 1)
                        if there(b, p, -1, first, last):
                            turn(*pair(b, p, 1))
                        if there(b, p, 1, first, last):
                            turn_p(*earlier(b, p, 1), 0)
                            turn_p(*earlier(b, p, 1), 1)
                        if p == 1 and not first:
                            project(b - 1)
                        if p + AHEAD < PAIRS:
                            qkv(b, p + AHEAD, xcur)
                        elif not last:
                            if p + AHEAD == PAIRS:
                                pe.wait_ge(xx, b + 1)
                            qkv(b + 1, p + AHEAD - PAIRS, xnext)
                        if p == 1 and not first:
                            pe.wait_ge(res, b)
                        if there(b, p, 1, first, last):
                            values(*earlier(b, p, 1))
                        if p == PAIRS - 1 and not last:
                            pe.wait_ge(xc, b + 2)

                pe.wait_ge(xc, 1)
                for p in range(AHEAD):
                    qkv(0, p, xcur)
                turn(0, 0)
                batch(0, True, False)
                with pe.Fori(1, BATCH - 1) as b:
                    batch(b, False, False)
                batch(BATCH - 1, False, True)
                for h in range(2):
                    turn_p(BATCH - 1, PAIRS - 1, h)
                values(BATCH - 1, PAIRS - 1)
                project(BATCH - 1)

            @block.vector
            def _(v):
                def rotate(b, p):
                    u = PAIRS * b + p
                    v.wait_ge(qk, u + 1)
                    after(v, tq, u - 1)
                    nc.vector.tensor_tensor(m1[:, p % 2, :], ps[:, QB, :], cos[:, :, :].rearrange("p t c -> p (t c)"),
                                            ALU.mult)
                    q = ps[:, QB, :].rearrange("p (h i s) -> p h s i", h=4 * TPB, s=2)
                    nc.vector.tensor_tensor(
                        m2[:, p % 2, :].rearrange("p (h s i) -> p h s i", h=4 * TPB, s=2), q[:, :, ::-1, :],
                        sin[:, :, :].rearrange("p t (h s i) -> p (t h) s i", h=4, s=2), ALU.mult).then_inc(rope, 1)

                def maximum(b, p, h):
                    u = PAIRS * b + p
                    v.wait_ge(sc, 2 * u + h + 1)
                    nc.vector.tensor_reduce(nmax[:, p % 2, h, :], ps[:, SB + h, :].rearrange("p (t k) -> p t k", t=TPB),
                                            AX.X, ALU.max, negate=True).then_inc(mx, 1)

                def normalise(b, p, h):
                    u = PAIRS * b + p
                    v.wait_ge(ex, 2 * u + h + 1)
                    nc.vector.reciprocal(rinv[:, p % 2, h, :], rsum[:, p % 2, h, :]).then_inc(rc, 1)
                    v.wait_ge(rc, 2 * u + h + 1)
                    for t in range(TPB):
                        mm = nc.vector.tensor_scalar(prob[:, p % 2, h, t, :], prob[:, p % 2, h, t, :],
                                                     rinv[:, p % 2, h, t:t + 1], None, ALU.mult)
                    mm.then_inc(pn, 1)

                def residual(b):
                    v.wait_ge(op, b + 1)
                    xs = x[:, bass.ds(TPB * b, TPB), :]
                    nc.vector.tensor_tensor(xs, ps[:, OB, 0:SEQ].rearrange("p (t d) -> p t d", t=TPB), xs,
                                            ALU.add).then_inc(res, 1)

                def batch(b, first, last):
                    for p in range(PAIRS):
                        if there(b, p, -2, first, last):
                            rotate(*pair(b, p, 2))
                        maximum(b, p, 0)
                        maximum(b, p, 1)
                        normalise(b, p, 0)
                        normalise(b, p, 1)
                        if p == 1 and not first:
                            residual(b - 1)

                rotate(0, 0)
                rotate(0, 1)
                batch(0, True, False)
                with v.Fori(1, BATCH - 1) as b:
                    batch(b, False, False)
                batch(BATCH - 1, False, True)
                residual(BATCH - 1)

            @block.scalar
            def _(act):
                def take_v(b, p):
                    u = PAIRS * b + p
                    act.wait_ge(vp, u + 1)
                    after(act, pv, 2 * (u - PAIRS + 1))
                    nc.scalar.copy(vsb[:, p, :, :].rearrange("p t d -> p (t d)"), ps[:, VB, 0:TPB * P]
                                   ).then_inc(vev, 1)

                def take_qk(b, p):
                    u = PAIRS * b + p
                    act.wait_ge(tq, u + 1)
                    after(act, sc, 2 * (u - 1))
                    nc.scalar.copy(qT[:, p % 2, :], ps[:, TB, 0:SEQ])
                    for h in range(2):
                        r = slice(h * DH, (h + 1) * DH)
                        mm = nc.scalar.copy(kT[r, p % 2, h, :], ps[r, TB, SEQ:])
                    mm.then_inc(qkev, 1)

                def exps(b, p, h):
                    u = PAIRS * b + p
                    act.wait_ge(mx, 2 * u + h + 1)
                    after(act, pt, 2 * (u - 2) + h + 1)
                    for t in range(TPB):
                        mm = nc.scalar.activation(prob[:, p % 2, h, t, :], ps[:, SB + h, t * SEQ:(t + 1) * SEQ],
                                                  ACT.Exp, bias=nmax[:, p % 2, h, t:t + 1],
                                                  accum_out=rsum[:, p % 2, h, t:t + 1])
                    mm.then_inc(ex, 1)

                def take_p(b, p, h):
                    u = PAIRS * b + p
                    act.wait_ge(pt, 2 * u + h + 1)
                    after(act, pv, 2 * (u - 1) + h + 1)
                    nc.scalar.copy(pT[:, h, :, :].rearrange("p j q -> p (j q)"), ps[:, PB + h, :]).then_inc(pte, 1)

                def take_o(b, p):
                    u = PAIRS * b + p
                    act.wait_ge(pv, 2 * u + 2)
                    if p == 0:
                        after(act, op, b)
                    nc.scalar.copy(oT[:, p, :], ps[:, OB, 0:SEQ]).then_inc(oev, 1)

                def batch(b, first, last):
                    for p in range(PAIRS):
                        if there(b, p, 2, first, last):
                            take_o(*earlier(b, p, 2))
                        exps(b, p, 0)
                        if there(b, p, -1, first, last):
                            take_qk(*pair(b, p, 1))
                        if there(b, p, 1, first, last):
                            take_p(*earlier(b, p, 1), 0)
                            take_p(*earlier(b, p, 1), 1)
                        exps(b, p, 1)
                        if there(b, p, -AHEAD, first, last):
                            take_v(*pair(b, p, AHEAD))

                act.wait_ge(z, 1)
                for p in range(AHEAD):
                    take_v(0, p)
                take_qk(0, 0)
                batch(0, True, False)
                with act.Fori(1, BATCH - 1) as b:
                    batch(b, False, False)
                batch(BATCH - 1, False, True)
                take_o(BATCH - 1, PAIRS - 2)
                for h in range(2):
                    take_p(BATCH - 1, PAIRS - 1, h)
                take_o(BATCH - 1, PAIRS - 1)


def build(nc, t, out):
    with ExitStack() as ctx:
        def sb(name, shape, dt=F32):
            return ctx.enter_context(nc.sbuf_tensor(name, shape, dt))

        ps = ctx.enter_context(nc.psum_tensor("ps", [P, 8, BLK], F32))
        x = sb("x", [P, TILES, DIM])
        ident = sb("ident", [P, P])
        iota_e = sb("iota_e", [P, EXPERTS], BF16)
        iota_p = sb("iota_p", [P, P, TOPK], BF16)
        iota_c = sb("iota_c", [P, COLS, TOPK], BF16)
        before = sb("before", [P, P], BF16)
        ones_bf = sb("ones_bf", [P, P], BF16)
        tokp1 = sb("tokp1", [P, TOPK], BF16)
        zeros = sb("zeros", [P, TOPK * DIM])
        xn_dram = nc.dram_tensor("xn_rows", [TOKENS, DIM], F32, kind="Internal").ap()
        y_dram = [nc.dram_tensor(f"y_rows{i}", [YROWS, DIM], F32, kind="Internal").ap() for i in range(2)]
        x_in = ctx.enter_context(nc.semaphore("x_in"))
        c0 = ctx.enter_context(nc.semaphore("c0"))
        with nc.Block() as block:
            @block.sync
            def _(sp):
                sp.dma_start(x[:, :, :], t["x"].rearrange("(t p) d -> p t d", p=P)).then_inc(x_in, 16)
                sp.wait_ge(x_in, 16)

            @block.vector
            def _(v):
                nc.vector.memset(zeros[:, :], 0.0)
                nc.vector.memset(ones_bf[:, :], 1.0)

            @block.gpsimd
            def _(pool):
                nc.gpsimd.memset(ident[:, :], 1.0).then_inc(c0, 1)
                nc.gpsimd.memset(before[:, :], 1.0).then_inc(c0, 1)
                nc.gpsimd.iota(iota_e[:, :], [[1, EXPERTS]], base=0, channel_multiplier=0,
                               allow_small_or_imprecise_dtypes=True)
                nc.gpsimd.iota(iota_p[:, :, :], [[1, P], [0, TOPK]], base=0, channel_multiplier=0,
                               allow_small_or_imprecise_dtypes=True)
                nc.gpsimd.iota(iota_c[:, :, :], [[1, COLS], [0, TOPK]], base=0, channel_multiplier=0,
                               allow_small_or_imprecise_dtypes=True)
                nc.gpsimd.iota(tokp1[:, :], [[0, TOPK]], base=1, channel_multiplier=1,
                               allow_small_or_imprecise_dtypes=True)
                pool.wait_ge(c0, 2)
                nc.gpsimd.affine_select(out=ident[:, :], in_=ident[:, :], compare_op=ALU.is_equal, fill=0.0, base=0,
                                        pattern=[[-1, P]], channel_multiplier=1)
                nc.gpsimd.affine_select(out=before[:, :], in_=before[:, :], compare_op=ALU.is_gt, fill=0.0, base=0,
                                        pattern=[[1, P]], channel_multiplier=-1)

        consts = (ident, iota_e, iota_p, iota_c, before, ones_bf, tokp1, zeros)
        fw = (t["wexp"], t["shw"], t["wg"])
        ffn(nc, x, consts, fw, y_dram[0], xn_dram, ps, "f1")
        attention(nc, x, (t["wqkv"], t["wout"], t["wf"], t["bf"], t["bo"], (t["cos"], t["sin"]), t["four"]),
                  consts, ps)
        ffn(nc, x, consts, fw, y_dram[1], xn_dram, ps, "f2", out_dram=out)


def tables():
    pos = np.arange(SEQ, dtype=np.float32)[:, None]
    freqs = np.float32(10000.0) ** (-np.arange(0, DH, 2, dtype=np.float32) / np.float32(DH))
    ang = np.repeat(pos * freqs.astype(np.float32), 2, axis=1)
    sin, cos = np.sin(ang), np.cos(ang)
    sign = np.where(np.arange(DH) < DH // 2, -1.0, 1.0).astype(np.float32)
    pf = pos * np.arange(1, FREQS + 1, dtype=np.float32)
    four = np.concatenate([np.sin(pf), np.cos(pf)], axis=1).T

    def tile(a):
        a = a.reshape(TPB, P, DH).transpose(1, 0, 2).astype(np.float32)
        return np.concatenate([np.float32(SCALE) * a] * 2 + [a] * 2, axis=2)
    return tile(cos), tile(sin * sign), np.ascontiguousarray(four).astype(np.float32)


def kernel(L0_attn_x, L0_attn_w_qkv, L0_attn_w_fproj, L0_attn_b_fproj, L0_attn_w_out, L0_attn_b_out, L0_ffn_wg,
           L0_ffn_shared_w1, L0_ffn_shared_w2, L0_ffn_expert_w1, L0_ffn_expert_w2):
    import concourse.bacc as bacc
    from concourse.bass_utils import run_bass_kernel_spmd

    def experts(w1, w2):
        a = np.asarray(w1).transpose(0, 2, 1)
        b = np.asarray(w2).transpose(0, 2, 1).reshape(-1, FC, P, DIM).transpose(0, 2, 1, 3).reshape(-1, P, FC * DIM)
        return np.ascontiguousarray(np.concatenate([a, b], axis=2))

    wqkv = np.asarray(L0_attn_w_qkv).reshape(3, PAIRS, P, DIM).transpose(3, 1, 0, 2).reshape(DIM, PAIRS, 3 * P)
    wout = np.asarray(L0_attn_w_out).T.reshape(PAIRS, P, DIM).transpose(1, 0, 2)
    wf = np.asarray(L0_attn_w_fproj).T
    bf = np.asarray(L0_attn_b_fproj)
    cos, sin, four = tables()
    arrays = {
        "x": np.asarray(L0_attn_x).reshape(TOKENS, DIM),
        "wexp": experts(L0_ffn_expert_w1, L0_ffn_expert_w2),
        "shw": experts(np.asarray(L0_ffn_shared_w1)[None], np.asarray(L0_ffn_shared_w2)[None])[0],
        "wg": np.asarray(L0_ffn_wg).T,
        "wqkv": wqkv, "wout": wout,
        "wf": np.concatenate([wf] * 4, axis=1), "bf": np.broadcast_to(np.concatenate([bf] * 4), (P, 4 * DH)),
        "bo": np.broadcast_to(np.asarray(L0_attn_b_out), (P, DIM)),
        "cos": cos, "sin": sin, "four": four,
    }
    arrays = {n: np.ascontiguousarray(a) for n, a in arrays.items()}
    nc = bacc.Bacc("TRN2", target_bir_lowering=False, num_devices=1)
    t = {n: nc.dram_tensor(f"in_{n}", a.shape, mybir.dt.from_np(a.dtype), kind="ExternalInput").ap()
         for n, a in arrays.items()}
    out = nc.dram_tensor("out", [TOKENS, DIM], F32, kind="ExternalOutput").ap()
    build(nc, t, out)
    r = run_bass_kernel_spmd(nc, [{f"in_{n}": a for n, a in arrays.items()}], core_ids=[0])
    return r.results[0]["out"].reshape(BATCH, SEQ, DIM)
```

```python
from contextlib import ExitStack

import numpy as np

import concourse.bass as bass
from concourse import mybir

F32 = mybir.dt.float32
F32R = mybir.dt.float32r
BF16 = mybir.dt.bfloat16
F16 = mybir.dt.float16
I32 = mybir.dt.int32
U32 = mybir.dt.uint32
ALU = mybir.AluOpType
ACT = mybir.ActivationFunctionType
AX = mybir.AxisListType

P = 128
BATCH, SEQ, DIM = 8, 256, 128
TOKENS = BATCH * SEQ
TILES = TOKENS // P
TPB = SEQ // P

HEADS, DH, FREQS = 16, 64, 16
INNER = HEADS * DH
PAIRS = HEADS // 2
SCALE = DH ** -0.5

EXPERTS, TOPK, FFN, CAPACITY = 64, 8, 384, 160
FC = FFN // P
WCOLS = 2 * FFN + FC * DIM
PLACES = EXPERTS * CAPACITY
COLS = PLACES // P
GE = 4
GT = GE * CAPACITY // P
GW = GE * CAPACITY
STEP_GROUPS = 2
STEP_EXPERTS = STEP_GROUPS * GE
STEPS = EXPERTS // STEP_EXPERTS
BLK = 512
BLOCKS = TOKENS // BLK
TPBLK = BLK // P
YROWS = TOKENS * TOPK
YB = 2
FAR = 32768.0
HIGH_BITS = -4096
EPS_LN = 1e-5
EPS_F32 = float(np.finfo(np.float32).eps)


def after(eng, sem, count):
    if not isinstance(count, int) or count > 0:
        eng.wait_ge(sem, count)


def product_3(nc, out, a, b):
    nc.tensor.matmul(out, a[0], b[0], start=True, stop=False)
    nc.tensor.matmul(out, a[0], b[1], start=False, stop=False)
    return nc.tensor.matmul(out, a[1], b[0], start=False, stop=True)


def experts(nc, x, wk, consts, w, ydram, xn_dram, ps, tag, clear_y, mv, known=0, split=None):
    wexp, shw, wg = w
    ident, iota_e, iota_p, iota_c, before, ones_bf, tokp1, zeros = consts
    with ExitStack() as ctx:
        def sb(name, shape, dt=F32):
            return ctx.enter_context(nc.sbuf_tensor(f"{tag}_{name}", shape, dt))

        def sem(name):
            return ctx.enter_context(nc.semaphore(f"{tag}_{name}"))

        ring = sb("ring", [P, STEP_EXPERTS, WCOLS])
        take = sb("take", [P, COLS], I32)
        put = sb("put", [P, COLS], I32)
        w_landed = [sem(f"w_landed{i}") for i in range(STEP_EXPERTS)]
        half_shared = sb("half_shared", [P, TILES, DIM])
        zeroed = sem("zeroed")
        xn_stored = sem("xn_stored")

        with ExitStack() as rctx:
            def rsb(name, shape, dt=F32):
                return rctx.enter_context(nc.sbuf_tensor(f"{tag}_{name}", shape, dt))

            def rsem(name):
                return rctx.enter_context(nc.semaphore(f"{tag}_{name}"))

            OHB = 4
            OT = TILES // OHB
            KBITS = (TOPK - 1).bit_length()
            xn = rsb("xn", [P, TILES, DIM])
            xnT = rsb("xnT", [P, TOKENS])
            bst = rsb("bst", [P, TILES, 6])
            st = rsb("st", [P, 2, TILES])
            pexp = rsb("pexp", [P, TILES])
            gate = rsb("gate", [P, TILES, EXPERTS])
            work = rsb("work", [P, TILES, EXPERTS])
            mask = rsb("mask", [P, TILES, EXPERTS], BF16)
            pre = rsb("pre", [P, 2, 8 + TILES, EXPERTS], BF16)
            top = rsb("top", [P, TILES, TOPK])
            topi = rsb("topi", [P, TILES, TOPK], U32)
            topf = rsb("topf", [P, TILES, TOPK])
            topr = rsb("topr", [P, TILES, TOPK, EXPERTS], F16)
            hit = rsb("hit", [P, TILES, TOPK, EXPERTS], F16)
            rank = rsb("rank", [P, TILES, EXPERTS], F16)
            rk = rsb("rk", [P, TILES, TOPK])
            sm = rsb("sm", [P, 3, TILES])
            far = rsb("far", [P, TILES, TOPK])
            pl = rsb("pl", [P, TILES, TOPK])
            pli = rsb("pli", [P, TILES * TOPK], I32)
            lo_i = rsb("lo_i", [P, 2, TILES * TOPK], I32)
            lo = rsb("lo", [P, 2, TILES, TOPK], F16)
            oh_p = rsb("oh_p", [P, OHB, P, TOPK], F16)
            oh_m = rsb("oh_m", [P, OHB, COLS, TOPK], F16)
            oh_t = rsb("oh_t", [P, OHB, COLS, TOPK], F16)
            tf = rsb("tf", [P, 1 + KBITS, COLS])
            tg = rsb("tg", [P, 4, COLS])
            sil = rsb("sil", [P, 2, BLK])
            hid = rsb("hid", [P, 2, FC, BLK])
            shsb = rsb("shsb", [P, WCOLS])
            wgsb = rsb("wgsb", [P, P])

            w_in = rsem("w_in")
            dv = rsem("dv")
            normed = rsem("normed")
            rstd = rsem("rstd")
            exped = rsem("exped")
            tps = rsem("tps")
            tsb = rsem("tsb")
            tsa = rsem("tsa")
            logit = rsem("logit")
            ranked = rsem("ranked")
            rank_in = rsem("rank_in")
            sh_h = rsem("sh_h")
            sh_c = rsem("sh_c")
            sh_a = rsem("sh_a")
            sh_o = rsem("sh_o")
            sh_x = rsem("sh_x")
            oh = rsem("oh")
            oh_a = rsem("oh_a")
            topr_in = rsem("topr_in")
            inv = rsem("inv")
            pconst = rsem("pconst")

            LOGB = (0, 1, 6, 7)
            RANKB, TRB, HB, OB, INVB = 0, 2, 2, 6, 7
            QUARTERS = 4
            QC = TILES * TOPK // QUARTERS
            QUARTERS_AFTER = {3: (0, 1), 4: (2,), 5: (3,)}

            VARIANCE, LESS_MAX, GATES, CHOSEN, SUMMED, PLACED = 3, 6, 9, 12, 18, 36

            with nc.Block() as block:
                @block.sync
                def _(sp):
                    sp.dma_start(shsb[:, :], shw).then_inc(w_in, 16)
                    sp.dma_start(wgsb[:, :], wg).then_inc(w_in, 16)
                    for e in range(STEP_EXPERTS):
                        sp.dma_start(ring[:, e, :], wexp[e]).then_inc(w_landed[e], 16)
                    sp.wait_ge(normed, BLOCKS)
                    sp.dma_start(xn_dram.rearrange("(t p) d -> p t d", p=P), xn[:, :, :]).then_inc(xn_stored, 16)
                    if clear_y:
                        y0 = ydram.rearrange("(c p r) d -> c p (r d)", p=P, r=TOPK)
                        for c in range(TILES):
                            sp.dma_start(y0[c], zeros[:, :]).then_inc(zeroed, 16)
                    sp.wait_ge(w_in, 32)

                @block.gpsimd
                def _(pool):
                    nc.gpsimd.memset(pexp[:, :], -0.5).then_inc(pconst, 1)
                    nc.gpsimd.memset(pre[:, :, 0:8, :], 0.0).then_inc(pconst, 1)
                    pool.wait_ge(pconst, 1)
                    pool.wait_ge(dv, VARIANCE)
                    nc.gpsimd.tensor_tensor(st[:, 1, :], st[:, 0, :], pexp[:, :], ALU.pow).then_inc(rstd, 1)
                    for c in range(FC * BLOCKS):
                        b, f = c // FC, c % FC
                        pool.wait_ge(sh_c, c + 1)
                        nc.gpsimd.tensor_tensor(hid[:, b % 2, f, :], hid[:, b % 2, f, :], sil[:, c % 2, :],
                                                ALU.mult).then_inc(sh_a, 1)

                @block.vector
                def _(v):
                    n = [0]

                    def step(ins):
                        n[0] += 1
                        ins.then_inc(dv, 1)
                        v.wait_ge(dv, n[0])

                    def bc(ap, m):
                        return ap.unsqueeze(2).to_broadcast([P, TILES, m])

                    for t in range(known, TILES):
                        last = nc.vector.bn_stats(bst[:, t, :], x[:, t, :])
                    step(last)
                    for t in range(known, TILES):
                        last = nc.vector.bn_aggr(mv[:, t, :], bst[:, t, :])
                    step(last)
                    step(nc.vector.tensor_scalar(st[:, 0, :], mv[:, :, 1], EPS_LN, None, ALU.add))
                    step(nc.vector.tensor_tensor(xn[:, :, :], x[:, :, :], bc(mv[:, :, 0], DIM), ALU.subtract))
                    v.wait_ge(rstd, 1)
                    for c in range(BLOCKS):
                        a = slice(c * TPBLK, (c + 1) * TPBLK)
                        nc.vector.tensor_tensor(xn[:, a, :], xn[:, a, :],
                                                st[:, 1, a].unsqueeze(2).to_broadcast([P, TPBLK, DIM]),
                                                ALU.mult).then_inc(normed, 1)
                    for c in range(0, BLOCKS, 2):
                        v.wait_ge(tps, c + 1)
                        nc.vector.tensor_copy(xnT[:, c * BLK:(c + 1) * BLK], ps[:, TRB + c, :]).then_inc(tsb, 1)
                    v.wait_ge(logit, 1)
                    lg = [(slice(8 * g, 8 * (g + 1)),
                           ps[:, b:b + 2, :].rearrange("p b (t e) -> p (b t) e", e=P)[:, :, 0:EXPERTS])
                          for g, b in enumerate(LOGB[0::2])]
                    for a, l in lg:
                        last = nc.vector.tensor_reduce(sm[:, 0, a], l, AX.X, ALU.max)
                    step(last)
                    for a, l in lg:
                        last = nc.vector.tensor_tensor(
                            work[:, a, :], l, sm[:, 0, a].unsqueeze(2).to_broadcast([P, 8, EXPERTS]), ALU.subtract)
                    step(last)
                    v.wait_ge(exped, 1)
                    step(nc.vector.tensor_reduce(sm[:, 1, :], gate[:, :, :], AX.X, ALU.add))
                    step(nc.vector.reciprocal(sm[:, 2, :], sm[:, 1, :]))
                    step(nc.vector.tensor_tensor(gate[:, :, :], gate[:, :, :], bc(sm[:, 2, :], EXPERTS), ALU.mult))
                    assert n[0] == GATES
                    for t in range(TILES):
                        last = nc.vector.max(top[:, t, :], gate[:, t, :])
                    step(last)
                    for t in range(TILES):
                        last = nc.vector.max_index(topi[:, t, :], top[:, t, :], gate[:, t, :])
                    step(last)
                    step(nc.vector.tensor_copy(topf[:, :, :], topi[:, :, :]))
                    assert n[0] == CHOSEN
                    for t in range(TILES):
                        last = nc.vector.match_replace(work[:, t, :], top[:, t, :], gate[:, t, :], -1.0)
                    step(last)
                    step(nc.vector.tensor_scalar(pre[:, 0, 8:, :], work[:, :, :], 0.0, None, ALU.is_lt))
                    nc.vector.tensor_copy(mask[:, :, :], pre[:, 0, 8:, :])
                    v.wait_ge(pconst, 2)
                    for i, s in enumerate((1, 2, 4, 8)):
                        a, b = i % 2, (i + 1) % 2
                        step(nc.vector.tensor_tensor(pre[:, b, 8:, :], pre[:, a, 8:, :],
                                                     pre[:, a, 8 - s:8 - s + TILES, :], ALU.add))
                    assert n[0] == SUMMED
                    step(nc.vector.tensor_reduce(sm[:, 0, :], top[:, :, :], AX.X, ALU.add))
                    step(nc.vector.tensor_scalar(sm[:, 0, :], sm[:, 0, :], EPS_F32, None, ALU.max))
                    step(nc.vector.reciprocal(sm[:, 1, :], sm[:, 0, :]))
                    step(nc.vector.scalar_tensor_tensor(wk[:, :, :], top[:, :, :], 0.5, bc(sm[:, 1, :], TOPK),
                                                        ALU.mult, ALU.mult))
                    hv = hit[:, :, :, :].rearrange("p t k e -> p (t k) e")
                    tv = topr[:, :, :, :].rearrange("p t k e -> p (t k) e")
                    for q in range(QUARTERS):
                        v.wait_ge(topr_in, q + 1)
                        last = nc.vector.tensor_tensor(
                            hv[:, q * QC:(q + 1) * QC], tv[:, q * QC:(q + 1) * QC],
                            iota_e[:, :].unsqueeze(1).to_broadcast([P, QC, EXPERTS]), ALU.is_equal)
                    step(last)
                    v.wait_ge(rank_in, 1)
                    step(nc.vector.tensor_tensor(hit[:, :, :, :], hit[:, :, :, :],
                                                 rank[:, :, :].unsqueeze(2).to_broadcast([P, TILES, TOPK, EXPERTS]),
                                                 ALU.mult))
                    half = EXPERTS // 2
                    while half >= 2:
                        step(nc.vector.tensor_tensor(hv[:, :, 0:half], hv[:, :, 0:half], hv[:, :, half:2 * half],
                                                     ALU.add))
                        half //= 2
                    step(nc.vector.tensor_tensor(rk[:, :, :].rearrange("p t k -> p (t k)"), hv[:, :, 0], hv[:, :, 1],
                                                 ALU.add))
                    step(nc.vector.tensor_scalar(far[:, :, :], rk[:, :, :], CAPACITY - 0.5, FAR, ALU.is_gt, ALU.mult))
                    step(nc.vector.scalar_tensor_tensor(wk[:, :, :], far[:, :, :], 0.5, wk[:, :, :],
                                                        ALU.is_lt, ALU.mult))
                    step(nc.vector.scalar_tensor_tensor(pl[:, :, :], topf[:, :, :], float(CAPACITY), rk[:, :, :],
                                                        ALU.mult, ALU.add))
                    step(nc.vector.tensor_tensor(pli[:, :], pl[:, :, :].rearrange("p t k -> p (t k)"),
                                                 far[:, :, :].rearrange("p t k -> p (t k)"), ALU.add))
                    nc.vector.tensor_scalar(lo_i[:, 0, :], pli[:, :], P - 1, None, ALU.bitwise_and)
                    step(nc.vector.tensor_scalar(lo_i[:, 1, :], pli[:, :], 7, None, ALU.logical_shift_right))
                    step(nc.vector.tensor_copy(lo[:, :, :, :].rearrange("p a t k -> p a (t k)"), lo_i[:, :, :]))
                    assert n[0] == PLACED
                    with v.Fori(0, OT) as i:
                        for h in range(OHB):
                            t = OHB * i + h
                            v.wait_ge(inv, t + 1)
                            lo_t = lo[:, :, bass.ds(t, 1), :]
                            nc.vector.tensor_tensor(oh_p[:, h, :, :], iota_p[:, :, :],
                                                    lo_t[:, 0, :, :].to_broadcast([P, P, TOPK]), ALU.is_equal)
                            nc.vector.tensor_tensor(oh_m[:, h, :, :], iota_c[:, :, :],
                                                    lo_t[:, 1, :, :].to_broadcast([P, COLS, TOPK]),
                                                    ALU.is_equal).then_inc(oh, 1)
                    v.wait_ge(inv, TILES + OHB)
                    step(nc.vector.tensor_copy(tf[:, :, :].rearrange("p a c -> p (a c)"),
                                               ps[:, INVB, 0:(1 + KBITS) * COLS]))
                    nc.vector.tensor_scalar(tg[:, 0, :], tf[:, 0, :], -1.0, None, ALU.add)
                    nc.vector.scalar_tensor_tensor(tg[:, 1, :], tf[:, 2, :], 2.0, tf[:, 1, :], ALU.mult, ALU.add)
                    step(nc.vector.tensor_scalar(tg[:, 2, :], tf[:, 0, :], 0.5, FAR, ALU.is_lt, ALU.mult))
                    nc.vector.tensor_scalar(take[:, :], tg[:, 0, :], 0.0, None, ALU.max)
                    nc.vector.scalar_tensor_tensor(tg[:, 3, :], tf[:, 3, :], 4.0, tg[:, 1, :], ALU.mult, ALU.add)
                    step(nc.vector.scalar_tensor_tensor(tg[:, 2, :], tg[:, 0, :], float(TOPK), tg[:, 2, :],
                                                        ALU.mult, ALU.add))
                    step(nc.vector.tensor_tensor(put[:, :], tg[:, 2, :], tg[:, 3, :], ALU.add))

                RANKS_AT = 6

                @block.tensor
                def _(pe):
                    for t in range(TILES):
                        if t % 4 == 0:
                            pe.wait_ge(normed, t // 4 + 1)
                        mm = nc.tensor.transpose(ps[:, TRB + t // 4, (t % 4) * P:(t % 4 + 1) * P], xn[:, t, :],
                                                 ident[:, :])
                        if t % 4 == 3:
                            mm.then_inc(tps, 1)
                    pe.wait_ge(w_in, 32)
                    for t in range(TILES):
                        if t % 8 == 0:
                            pe.wait_ge(tsb, t // 8 + 1)
                        if t % 8 == 4:
                            pe.wait_ge(tsa, t // 8 + 1)
                        mm = nc.tensor.matmul(ps[:, LOGB[t // 4], (t % 4) * P:(t % 4 + 1) * P],
                                              xnT[:, t * P:(t + 1) * P], wgsb[:, :], start=True, stop=True)
                    mm.then_inc(logit, 1)

                    def clear():
                        pe.wait_ge(dv, LESS_MAX)
                        nc.tensor.matmul(ps[:, INVB, 0:(1 + KBITS) * COLS], zeros[:, 0:P // 2].bitcast(F16),
                                         zeros[:, 0:(1 + KBITS) * COLS // 2].bitcast(F16), start=True, stop=True
                                         ).then_inc(inv, OHB)

                    def up(c):
                        b, f, h = c // FC, c % FC, c % 2
                        if c == 0:
                            pe.wait_ge(tsb, BLOCKS // 2)
                            pe.wait_ge(tsa, BLOCKS // 2)
                        if c >= 2:
                            pe.wait_ge(sh_c, c - 1)
                        for half in range(2):
                            mm = nc.tensor.matmul(ps[:, HB + 2 * h + half, :],
                                                  shsb[:, half * FFN + f * P:half * FFN + (f + 1) * P],
                                                  xnT[:, b * BLK:(b + 1) * BLK], start=True, stop=True)
                        mm.then_inc(sh_h, 1)

                    def down(b):
                        pe.wait_ge(sh_a, FC * (b + 1))
                        if b >= 1:
                            pe.wait_ge(sh_x, b)
                        for j in range(BLK // P):
                            for f in range(FC):
                                mm = nc.tensor.matmul(ps[:, OB, j * P:(j + 1) * P],
                                                      hid[:, b % 2, f, j * P:(j + 1) * P],
                                                      shsb[:, 2 * FFN + f * DIM:2 * FFN + (f + 1) * DIM],
                                                      start=(f == 0), stop=(f == FC - 1))
                        mm.then_inc(sh_o, 1)

                    def ranks():
                        pe.wait_ge(dv, SUMMED)
                        for t in range(TILES):
                            o = ps[:, RANKB + t // 8, (t % 8) * EXPERTS:(t % 8 + 1) * EXPERTS]
                            mm = nc.tensor.matmul(o, before[:, :], mask[:, t, :], start=True, stop=(t == 0))
                            if t:
                                mm = nc.tensor.matmul(o, ones_bf[:, :], pre[:, 0, 8 + t - 1, :],
                                                      start=False, stop=True)
                        mm.then_inc(ranked, 1)

                    def invert(i):
                        for h in range(OHB):
                            pe.wait_ge(oh, OHB * i + h + 1)
                            pe.wait_ge(oh_a, OHB * i + h + 1)
                            for k in range(TOPK):
                                mm = nc.tensor.matmul(ps[:, INVB, 0:COLS], oh_p[:, h, :, k], oh_t[:, h, :, k],
                                                      start=False, stop=False, skip_group_check=True)
                                for bit in range(KBITS):
                                    if k >> bit & 1:
                                        a = (1 + bit) * COLS
                                        mm = nc.tensor.matmul(ps[:, INVB, a:a + COLS], oh_p[:, h, :, k],
                                                              oh_m[:, h, :, k], start=False, stop=False,
                                                              skip_group_check=True)
                            mm.then_inc(inv, 1)

                    for c in range(FC * BLOCKS):
                        up(c)
                        if c == 1:
                            clear()
                        if c == RANKS_AT:
                            ranks()
                        if c % FC == 0 and c:
                            down(c // FC - 1)
                    with pe.Fori(0, OT) as i:
                        invert(i)
                    down(BLOCKS - 1)

                @block.scalar
                def _(act):
                    for c in range(1, BLOCKS, 2):
                        act.wait_ge(tps, c + 1)
                        nc.scalar.copy(xnT[:, c * BLK:(c + 1) * BLK], ps[:, TRB + c, :]).then_inc(tsa, 1)
                    act.wait_ge(dv, LESS_MAX)
                    nc.scalar.activation(gate[:, :, :], work[:, :, :], ACT.Exp).then_inc(exped, 1)

                    def repeat(q):
                        act.wait_ge(dv, CHOSEN)
                        nc.scalar.copy(
                            topr[:, :, :, :].rearrange("p t k e -> p (t k) e")[:, q * QC:(q + 1) * QC],
                            topf[:, :, :].rearrange("p t k -> p (t k)")[:, q * QC:(q + 1) * QC].unsqueeze(
                                2).to_broadcast([P, QC, EXPERTS])).then_inc(topr_in, 1)

                    def half_down(b):
                        act.wait_ge(sh_o, b + 1)
                        nc.scalar.mul(half_shared[:, b * 4:(b + 1) * 4, :].rearrange("p t d -> p (t d)"), ps[:, OB, :],
                                      0.5).then_inc(sh_x, 1)

                    for c in range(FC * BLOCKS):
                        b, f = c // FC, c % FC
                        act.wait_ge(sh_h, c + 1)
                        if c >= 2:
                            act.wait_ge(sh_a, c - 1)
                        nc.scalar.activation(sil[:, c % 2, :], ps[:, HB + 2 * (c % 2) + 1, :], ACT.Silu)
                        if b >= 2:
                            act.wait_ge(sh_o, b - 1)
                        nc.scalar.copy(hid[:, b % 2, f, :], ps[:, HB + 2 * (c % 2), :]).then_inc(sh_c, 1)
                        for q in QUARTERS_AFTER.get(c, ()):
                            repeat(q)
                        if c == RANKS_AT - 1:
                            act.wait_ge(ranked, 1)
                            nc.scalar.copy(rank[:, :, :].rearrange("p t e -> p (t e)"),
                                           ps[:, RANKB:RANKB + 2, :].rearrange("p b c -> p (b c)")
                                           ).then_inc(rank_in, 1)
                        if c % FC == FC - 1 and b >= 1:
                            half_down(b - 1)
                    def one_hot_tokens(i):
                        for h in range(OHB):
                            act.wait_ge(oh, OHB * i + h + 1)
                            nc.scalar.mul(oh_t[:, h, :, :], oh_m[:, h, :, :], tokp1[:, bass.ds(OHB * i + h, 1)]
                                          ).then_inc(oh_a, 1)

                    with act.Fori(0, OT) as i:
                        one_hot_tokens(i)
                    half_down(BLOCKS - 1)

        with ExitStack() as ectx:
            def esb(name, shape, dt=F32):
                return ectx.enter_context(nc.sbuf_tensor(f"{tag}_{name}", shape, dt))

            def esem(name):
                return ectx.enter_context(nc.semaphore(f"{tag}_{name}"))

            SG = STEP_GROUPS
            tk = esb("tk", [P, SG, GT], I32)
            pt = esb("pt", [P, SG, GT], I32)
            xg = esb("xg", [P, SG, GT, DIM])
            xgT = esb("xgT", [P, SG, GW])
            sil = esb("esil", [P, 2, FC * CAPACITY])
            hid = esb("ehid", [P, 2, FC * CAPACITY])
            oT = esb("oT", [P, SG, GW])
            og = esb("og", [P, SG, GT, DIM])

            if split is not None:
                later_dram, high, low = split
                later = esb("later", high.shape)
                later_top = esb("later_top", high.shape)
                later_in = esem("later_in")
                later_cut = esem("later_cut")

            passed = esem("passed")
            tk_in = esem("tk_in")
            pt_in = esem("pt_in")
            got = [esem(f"got{g}") for g in range(SG)]
            sent = [esem(f"sent{g}") for g in range(SG)]
            xg_t = esem("xg_t")
            xg_s = esem("xg_s")
            hb = esem("hb")
            sl = esem("sl")
            ac = esem("ac")
            ob = esem("ob")
            os_ = esem("os")
            og_t = esem("og_t")
            og_s = esem("og_s")
            XB, HB, OB, GB = 0, 2, 6, 7

            with nc.Block() as block:
                @block.sync
                def _(sp):
                    if split is not None:
                        sp.wait_ge(hb, 1)
                        sp.dma_start(later[:, :], later_dram).then_inc(later_in, 16)
                    with sp.Fori(1, STEPS) as i:
                        for e in range(STEP_EXPERTS):
                            sp.wait_ge(ob, STEP_EXPERTS * (i - 1) + e + 1)
                            sp.dma_start(ring[:, e, :], wexp[bass.ds(STEP_EXPERTS * i + e, 1), :, :].rearrange(
                                "e p c -> (e p) c")).then_inc(w_landed[e], 16)

                @block.gpsimd
                def _(pool):
                    def gather(i, g):
                        G = SG * i + g
                        after(pool, xg_t, G - 1)
                        pool.wait_ge(xn_stored, 16)
                        nc.gpsimd.tensor_copy(tk[:, g, :], take[:, bass.ds(G * GT, GT)]).then_inc(tk_in, 1)
                        pool.wait_ge(tk_in, G + 1)
                        pool.sem_inc(passed, 1)
                        for s in range(GT):
                            nc.gpsimd.indirect_dma_start(
                                xg[:, g, s, :], None, xn_dram, bass.IndirectOffsetOnAxis(tk[:, g, s:s + 1], 0),
                                bounds_check=TOKENS - 1, oob_is_err=False).then_inc(got[g], 16)

                    def scatter(i, g):
                        G = SG * i + g
                        after(pool, sent[g], 16 * GT * i)
                        if clear_y:
                            pool.wait_ge(zeroed, 16 * TILES)
                        nc.gpsimd.tensor_copy(pt[:, g, :], put[:, bass.ds(G * GT, GT)]).then_inc(pt_in, 1)
                        pool.wait_ge(pt_in, G + 1)
                        for s in range(GT):
                            if s in (0, 3):
                                pool.wait_ge(og_s, 2 * G + 1 + s // 3)
                                pool.sem_inc(passed, 1)
                            nc.gpsimd.indirect_dma_start(
                                ydram, bass.IndirectOffsetOnAxis(pt[:, g, s:s + 1], 0), og[:, g, s, :], None,
                                bounds_check=YROWS - 1, oob_is_err=False).then_inc(sent[g], 16)

                    for g in range(SG):
                        gather(0, g)
                    for g in range(SG):
                        gather(1, g)
                    for g in range(SG):
                        scatter(0, g)
                        gather(2, g)
                    with pool.Fori(3, STEPS) as i:
                        for g in range(SG):
                            scatter(i - 2, g)
                            gather(i, g)
                    for i in (STEPS - 2, STEPS - 1):
                        for g in range(SG):
                            scatter(i, g)
                    for g in range(SG):
                        pool.wait_ge(sent[g], 16 * GT * STEPS)

                @block.tensor
                def _(pe):
                    def turn_in(i, g):
                        G = SG * i + g
                        after(pe, xg_s, G)
                        pe.wait_ge(got[g], 16 * GT * i + 16 * GT)
                        for s in range(GT):
                            mm = nc.tensor.transpose(ps[:, XB + s // 4, (s % 4) * P:(s % 4 + 1) * P],
                                                     xg[:, g, s, :], ident[:, :])
                        mm.then_inc(xg_t, 1)

                    def up(i, e):
                        g, E = e // GE, STEP_EXPERTS * i + e
                        pe.wait_ge(w_landed[e], 16 * i + 16)
                        if e % GE == 0:
                            pe.wait_ge(xg_s, SG * i + g + 1)
                        after(pe, ac, E - 1)
                        a = (e % GE) * CAPACITY
                        for half in range(2):
                            for f in range(FC):
                                mm = nc.tensor.matmul(
                                    ps[:, HB + 2 * (e % 2) + half, f * CAPACITY:(f + 1) * CAPACITY],
                                    ring[:, e, half * FFN + f * P:half * FFN + (f + 1) * P],
                                    xgT[:, g, a:a + CAPACITY], start=True, stop=True)
                        mm.then_inc(hb, 1)

                    def down(i, e):
                        E = STEP_EXPERTS * i + e
                        pe.wait_ge(ac, E + 1)
                        after(pe, os_, E)
                        for f in range(FC):
                            mm = nc.tensor.matmul(ps[:, OB, 0:CAPACITY],
                                                  ring[:, e, 2 * FFN + f * DIM:2 * FFN + (f + 1) * DIM],
                                                  hid[:, e % 2, f * CAPACITY:(f + 1) * CAPACITY],
                                                  start=(f == 0), stop=(f == FC - 1))
                        mm.then_inc(ob, 1)

                    def turn_out(i, g, part):
                        G = SG * i + g
                        pe.wait_ge(os_, GE * (G + 1))
                        after(pe, og_s, 2 * G + part)
                        for s in range(3) if part == 0 else range(3, GT):
                            mm = nc.tensor.transpose(ps[:, GB, (s % 3) * P:(s % 3 + 1) * P],
                                                     oT[:, g, s * P:(s + 1) * P], ident[:, :])
                        mm.then_inc(og_t, 1)

                    def step(i, first, last):
                        for e in range(STEP_EXPERTS):
                            g, r = e // GE, e % GE
                            if r == 2 and not (last and g == SG - 1):
                                turn_in(*((i, g + 1) if g < SG - 1 else (i + 1, 0)))
                            if e < STEP_EXPERTS - 1:
                                up(i, e + 1)
                            elif not last:
                                up(i + 1, 0)
                            down(i, e)
                            if r in (0, 1) and not (first and g == 0):
                                turn_out(*((i, g - 1) if g else (i - 1, SG - 1)), r)

                    turn_in(0, 0)
                    up(0, 0)
                    step(0, True, False)
                    step(1, False, False)
                    with pe.Fori(2, STEPS - 1) as i:
                        step(i, False, False)
                    step(STEPS - 1, False, True)
                    turn_out(STEPS - 1, SG - 1, 0)
                    turn_out(STEPS - 1, SG - 1, 1)

                @block.scalar
                def _(act):
                    def group_in(i, g):
                        G = SG * i + g
                        act.wait_ge(xg_t, G + 1)
                        after(act, hb, GE * (G - 1))
                        nc.scalar.copy(xgT[:, g, :], ps[:, XB:XB + 2, :].rearrange("p b c -> p (b c)")[:, 0:GW]
                                       ).then_inc(xg_s, 1)

                    def silu(i, e):
                        E = STEP_EXPERTS * i + e
                        act.wait_ge(hb, E + 1)
                        after(act, ac, E - 1)
                        nc.scalar.activation(sil[:, e % 2, :], ps[:, HB + 2 * (e % 2) + 1, 0:FC * CAPACITY],
                                             ACT.Silu).then_inc(sl, 1)

                    def group_out(i, g, part):
                        G = SG * i + g
                        act.wait_ge(og_t, 2 * G + part + 1)
                        if part == 0:
                            after(act, sent[g], 16 * GT * i)
                        a, b = ((0, 3), (3, GT))[part]
                        nc.scalar.copy(og[:, g, a:b, :].rearrange("p s d -> p (s d)"),
                                       ps[:, GB, 0:(b - a) * P]).then_inc(og_s, 1)

                    def step(i, first, last):
                        for e in range(STEP_EXPERTS):
                            g, r = e // GE, e % GE
                            if r == 2 and not (last and g == SG - 1):
                                group_in(*((i, g + 1) if g < SG - 1 else (i + 1, 0)))
                            if e < STEP_EXPERTS - 1:
                                silu(i, e + 1)
                            elif not last:
                                silu(i + 1, 0)
                            if r in (0, 1) and not (first and g == 0):
                                group_out(*((i, g - 1) if g else (i - 1, SG - 1)), r)

                    group_in(0, 0)
                    silu(0, 0)
                    step(0, True, False)
                    step(1, False, False)
                    with act.Fori(2, STEPS - 1) as i:
                        step(i, False, False)
                    step(STEPS - 1, False, True)
                    group_out(STEPS - 1, SG - 1, 0)
                    group_out(STEPS - 1, SG - 1, 1)

                @block.vector
                def _(v):
                    def split_piece(e):
                        w = high.shape[1] // STEP_EXPERTS
                        a = slice(e * w, (e + 1) * w)
                        v.wait_ge(later_in, 16)
                        nc.vector.tensor_scalar(later_top[:, a].bitcast(I32), later[:, a].bitcast(I32), HIGH_BITS,
                                                None, ALU.bitwise_and).then_inc(later_cut, 1)
                        v.wait_ge(later_cut, e + 1)
                        nc.vector.tensor_copy(high[:, a], later_top[:, a])
                        nc.vector.tensor_tensor(low[:, a], later[:, a], later_top[:, a], ALU.subtract)

                    nc.vector.tensor_tensor(x[:, :, :], x[:, :, :], half_shared[:, :, :], ALU.add)

                    def product(i, e):
                        E = STEP_EXPERTS * i + e
                        v.wait_ge(sl, E + 1)
                        after(v, ob, E - 1)
                        nc.vector.tensor_tensor(hid[:, e % 2, :], sil[:, e % 2, :],
                                                ps[:, HB + 2 * (e % 2), 0:FC * CAPACITY], ALU.mult).then_inc(ac, 1)

                    def output(i, e):
                        g, E = e // GE, STEP_EXPERTS * i + e
                        v.wait_ge(ob, E + 1)
                        if e % GE == 0:
                            after(v, og_t, 2 * (SG * i + g - 1))
                        a = (e % GE) * CAPACITY
                        nc.vector.tensor_copy(oT[:, g, a:a + CAPACITY], ps[:, OB, 0:CAPACITY]).then_inc(os_, 1)

                    def step(i, first, last):
                        for e in range(STEP_EXPERTS):
                            if e < STEP_EXPERTS - 1:
                                product(i, e + 1)
                            elif not last:
                                product(i + 1, 0)
                            output(i, e)
                            if first and split is not None:
                                split_piece(e)

                    product(0, 0)
                    step(0, True, False)
                    step(1, False, False)
                    with v.Fori(2, STEPS - 1) as i:
                        step(i, False, False)
                    step(STEPS - 1, False, True)


def weighted_sum(nc, x, wk, ident, ydram, out_dram, ps):
    with ExitStack() as ctx:
        QS = TILES // YB
        yt = ctx.enter_context(nc.sbuf_tensor("ws_yt", [P, TILES, TOPK * DIM], F32))
        z = ctx.enter_context(nc.sbuf_tensor("ws_z", [P, 2, TOPK, YB, DIM], F32))
        y_in = [ctx.enter_context(nc.semaphore(f"ws_y_in{q}")) for q in range(QS)]
        summed = ctx.enter_context(nc.semaphore("ws_summed"))
        scaled = ctx.enter_context(nc.semaphore("ws_scaled"))
        psum = ctx.enter_context(nc.semaphore("ws_psum"))
        joined = ctx.enter_context(nc.semaphore("ws_joined"))
        stored = ctx.enter_context(nc.semaphore("ws_stored"))
        ysrc = ydram.rearrange("(c p r) d -> p c (r d)", p=P, r=TOPK)
        dst = out_dram.rearrange("(t p) d -> p t d", p=P)
        with nc.Block() as block:
            @block.sync
            def _(sp):
                for q in range(QS):
                    sp.dma_start(yt[:, q * YB:(q + 1) * YB, :], ysrc[:, q * YB:(q + 1) * YB, :]).then_inc(y_in[q], 16)
                for q in range(QS):
                    if q % 2 == 0:
                        sp.wait_ge(summed, TOPK * (q // 2 + 1))
                    else:
                        sp.wait_ge(joined, q // 2 + 1)
                    sp.dma_start(dst[:, q * YB:(q + 1) * YB, :], x[:, q * YB:(q + 1) * YB, :]).then_inc(stored, 16)
                sp.wait_ge(stored, 16 * QS)

            @block.vector
            def _(v):
                def join(m):
                    q = 2 * m + 1
                    v.wait_ge(psum, m + 1)
                    xs = x[:, q * YB:(q + 1) * YB, :]
                    nc.vector.tensor_tensor(xs, xs, ps[:, m % 2, 0:YB * DIM].rearrange("p (t d) -> p t d", t=YB),
                                            ALU.add).then_inc(joined, 1)

                n = 0
                for m in range(QS // 2):
                    q = 2 * m
                    v.wait_ge(y_in[q], 16)
                    for k in range(TOPK):
                        if k:
                            v.wait_ge(summed, n)
                        for t in range(q * YB, (q + 1) * YB):
                            last = nc.vector.scalar_tensor_tensor(
                                x[:, t, :], yt[:, t, k * DIM:(k + 1) * DIM], wk[:, t, k:k + 1], x[:, t, :],
                                ALU.mult, ALU.add)
                        n += 1
                        last.then_inc(summed, 1)
                    if m:
                        join(m - 1)
                join(QS // 2 - 1)

            @block.scalar
            def _(act):
                for m in range(QS // 2):
                    q = 2 * m + 1
                    act.wait_ge(y_in[q], 16)
                    if m >= 2:
                        act.wait_ge(psum, m - 1)
                    for k in range(TOPK):
                        for j in range(YB):
                            t = q * YB + j
                            last = nc.scalar.mul(z[:, m % 2, k, j, :], yt[:, t, k * DIM:(k + 1) * DIM],
                                                 wk[:, t, k:k + 1])
                        last.then_inc(scaled, 1)

            @block.tensor
            def _(pe):
                for m in range(QS // 2):
                    if m >= 2:
                        pe.wait_ge(joined, m - 1)
                    for k in range(TOPK):
                        pe.wait_ge(scaled, TOPK * m + k + 1)
                        mm = nc.tensor.matmul(ps[:, m % 2, 0:YB * DIM], ident[:, :],
                                              z[:, m % 2, k, :, :].rearrange("p t d -> p (t d)"),
                                              start=(k == 0), stop=(k == TOPK - 1))
                    mm.then_inc(psum, 1)


def attention(nc, x, wk, ydram, attn_w, consts, ps, mv_out):
    (wqh, wql), wv, wout, wf, bf, bo, tabs, four = attn_w
    ident = consts[0]
    with ExitStack() as ctx:
        def sb(name, shape, dt=F32):
            return ctx.enter_context(nc.sbuf_tensor(f"at_{name}", shape, dt))

        def sem(name):
            return ctx.enter_context(nc.semaphore(f"at_{name}"))

        QKW = 2 * P
        wv_sb = sb("wv", [P, PAIRS, P])
        wo_sb = sb("wout", [P, PAIRS, DIM])
        wf_sb = sb("wf", [2 * FREQS, QKW])
        four_sb = sb("four", [2 * FREQS, SEQ])
        bf_sb = sb("bf", [P, QKW])
        bo_sb = sb("bo", [P, DIM])
        cos = sb("cos", [P, TPB, QKW])
        sin = sb("sin", [P, TPB, QKW])
        fenc = sb("fenc", [P, TPB, QKW])
        xcur = sb("xcur", [P, 2, SEQ], F32R)
        xnext = sb("xnext", [P, 2, SEQ], F32R)
        xnew = sb("xnew", [P, SEQ])
        xwhole = sb("xwhole", [P, SEQ])
        xtop = sb("xtop", [P, SEQ])
        xn = sb("xn", [P, TPB, DIM])
        yt = sb("yt", [P, TILES, TOPK * DIM])
        bst = sb("bst", [P, TPB, 6])
        mv = sb("mv", [P, TPB, 2])
        st = sb("st", [P, 2, TPB])
        pexp = sb("pexp", [P, TPB])

        m1 = sb("m1", [P, 2, TPB * QKW])
        m2 = sb("m2", [P, 2, TPB * QKW])
        vsb = sb("v", [P, PAIRS, TPB, P])
        qT = sb("qT", [P, 2, SEQ])
        kT = sb("kT", [P, 2, 2, SEQ])
        nmax = sb("nmax", [P, 2, 2, TPB])
        rsum = sb("rsum", [P, 2, 2, TPB])
        rinv = sb("rinv", [P, 2, 2, TPB])
        prob = sb("prob", [P, 2, 2, TPB, SEQ])
        pT = sb("pT", [P, 2, TPB, SEQ])
        oT = sb("oTh", [P, PAIRS, SEQ])

        passed, passed_v = sem("passed"), sem("passed_v")
        loaded, fe, fs, const = sem("loaded"), sem("fe"), sem("fs"), sem("const")
        y_in, summed = sem("y_in"), sem("summed")
        bn, agg, var, rstd = sem("bn"), sem("agg"), sem("var"), sem("rstd")
        xnd, biased, xt = sem("xnd"), sem("biased"), sem("xt")
        xev, xh = sem("xev"), sem("xh")
        xc, xx = sem("xc"), sem("xx")
        qk, vp = sem("qk"), sem("vp")
        rope, fadd, msum = sem("rope"), sem("fadd"), sem("msum")
        vev, tq = sem("vev"), sem("tq")
        qkev = sem("qkev")
        sc, mx, ex = sem("sc"), sem("mx"), sem("ex")
        rc, pn = sem("rc"), sem("pn")
        pt, pte = sem("pt"), sem("pte")
        pv, oev = sem("pv"), sem("oev")
        op, res, z = sem("op"), sem("res"), sem("z")
        QB, VB, TB, SB, PB, OB = 0, 1, 2, 3, 5, 7
        AHEAD = 3

        def pair(b, p, ahead):
            return (b, p + ahead) if p + ahead < PAIRS else (b + 1, p + ahead - PAIRS)

        def earlier(b, p, back):
            return (b, p - back) if p >= back else (b - 1, p - back + PAIRS)

        def there(b, p, back, first, last):
            return not (first and p - back < 0) and not (last and p - back >= PAIRS)

        LN_STATS, LN_MEAN, LN_APPLY, LN_BIAS = 0, 1, 2, 3
        LN_TURN = 3
        LOADS = 8

        with nc.Block() as block:
            @block.sync
            def _(sp):
                ysrc = ydram.rearrange("(c p r) d -> p c (r d)", p=P, r=TOPK)
                for b in range(BATCH):
                    ts = slice(TPB * b, TPB * (b + 1))
                    sp.dma_start(yt[:, ts, :], ysrc[:, ts, :]).then_inc(y_in, 16)
                    sp.wait_ge(y_in, 16 * (b + 1))

            @block.gpsimd
            def _(pool):
                nc.gpsimd.memset(pexp[:, :], -0.5).then_inc(const, 1)
                pool.wait_ge(const, 1)
                nc.gpsimd.memset(kT[:, :, :, :], 0.0).then_inc(z, 1)

                def load_cur(b):
                    after(pool, vp, PAIRS * b)
                    pool.wait_ge(xx, b + 1)
                    pool.sem_inc(passed, 1)
                    nc.gpsimd.tensor_copy(xwhole[:, :], xnew[:, :])
                    nc.gpsimd.tensor_copy(xcur[:, :, :], xnext[:, :, :]).then_inc(xc, 1)

                def root(b):
                    pool.wait_ge(var, b + 1)
                    nc.gpsimd.tensor_tensor(st[:, 1, :], st[:, 0, :], pexp[:, :], ALU.pow).then_inc(rstd, 1)

                def add(b, p):
                    u = PAIRS * b + p
                    if isinstance(u, int) and u == 0:
                        pool.wait_ge(fs, 2)
                    pool.wait_ge(rope, u + 1)
                    nc.gpsimd.tensor_tensor(m1[:, p % 2, :], m1[:, p % 2, :], m2[:, p % 2, :],
                                            ALU.add).then_inc(fadd, 1)
                    pool.wait_ge(fadd, u + 1)
                    nc.gpsimd.tensor_tensor(m1[:, p % 2, :], m1[:, p % 2, :],
                                            fenc[:, :, :].rearrange("p t c -> p (t c)"), ALU.add).then_inc(msum, 1)

                def batch(b, last):
                    for p in range(PAIRS):
                        if there(b, p, -2, False, last):
                            add(*pair(b, p, 2))
                        if p == LN_MEAN and not last:
                            root(b + 1)
                        if p == PAIRS - AHEAD and not last:
                            load_cur(b + 1)

                root(0)
                load_cur(0)
                add(0, 0)
                add(0, 1)
                batch(0, False)
                with pool.Fori(1, BATCH - 1) as b:
                    batch(b, False)
                batch(BATCH - 1, True)

            @block.tensor
            def _(pe):
                def qkv(b, p, xs, whole, turned=None):
                    u = PAIRS * b + p
                    after(pe, rope, u)
                    for t in range(TPB):
                        x_parts = [xs[:, a, t * P:(t + 1) * P] for a in range(2)]
                        mm = product_3(nc, ps[:, QB, t * QKW:(t + 1) * QKW], x_parts,
                                       (wqh[:, p, :], wql[:, p, :]))
                    mm.then_inc(qk, 1)
                    after(pe, vev, u)
                    if p == (AHEAD + LN_TURN) % PAIRS and turned is not None:
                        pe.wait_ge(xev, turned)
                    for t in range(TPB):
                        mm = nc.tensor.matmul(ps[:, VB, t * P:(t + 1) * P], whole[:, t * P:(t + 1) * P],
                                              wv_sb[:, p, :], start=True, stop=True)
                    mm.then_inc(vp, 1)

                def turn_x(b, v_taken):
                    pe.wait_ge(xnd, b + 1)
                    after(pe, vev, v_taken)
                    for t in range(TPB):
                        mm = nc.tensor.transpose(ps[:, VB, SEQ + t * P:SEQ + (t + 1) * P], xn[:, t, :], ident[:, :])
                    mm.then_inc(xt, 1)

                def turn(b, p):
                    u = PAIRS * b + p
                    pe.wait_ge(msum, u + 1)
                    after(pe, qkev, u)
                    for half in range(2):
                        for t in range(TPB):
                            mm = nc.tensor.transpose(ps[:, TB, half * SEQ + t * P:half * SEQ + (t + 1) * P],
                                                     m1[:, p % 2, t * QKW + half * P:t * QKW + (half + 1) * P],
                                                     ident[:, :])
                    mm.then_inc(tq, 1)

                def scores(b, p, h):
                    u = PAIRS * b + p
                    if h == 0:
                        pe.wait_ge(qkev, u + 1)
                    after(pe, ex, 2 * u + h - 1)
                    for t in range(TPB):
                        mm = nc.tensor.matmul(ps[:, SB + h, t * SEQ:(t + 1) * SEQ], qT[:, p % 2, t * P:(t + 1) * P],
                                              kT[:, p % 2, h, :], start=True, stop=True)
                    mm.then_inc(sc, 1)

                def turn_p(b, p, h):
                    u = PAIRS * b + p
                    pe.wait_ge(pn, 2 * u + h + 1)
                    after(pe, pte, 2 * u + h - 1)
                    for t in range(TPB):
                        for j in range(TPB):
                            mm = nc.tensor.transpose(ps[:, PB + h, j * SEQ + t * P:j * SEQ + (t + 1) * P],
                                                     prob[:, p % 2, h, t, j * P:(j + 1) * P], ident[:, :])
                    mm.then_inc(pt, 1)

                def values(b, p):
                    u = PAIRS * b + p
                    pe.wait_ge(vev, u + 1)
                    after(pe, oev, u)
                    for h in range(2):
                        pe.wait_ge(pte, 2 * u + h + 1)
                        for j in range(TPB):
                            mm = nc.tensor.matmul(ps[h * DH:(h + 1) * DH, OB, 0:SEQ],
                                                  vsb[:, p, j, h * DH:(h + 1) * DH], pT[:, h, j, :],
                                                  start=(j == 0), stop=(j == TPB - 1))
                        mm.then_inc(pv, 1)

                def project(b):
                    pe.wait_ge(oev, PAIRS * (b + 1))
                    for t in range(TPB):
                        for p in range(PAIRS):
                            mm = nc.tensor.matmul(ps[:, OB, t * DIM:(t + 1) * DIM],
                                                  oT[:, p, t * P:(t + 1) * P], wo_sb[:, p, :],
                                                  start=(p == 0), stop=(p == PAIRS - 1))
                    mm.then_inc(op, 1)

                def batch(b, first, last):
                    for p in range(PAIRS):
                        scores(b, p, 0)
                        scores(b, p, 1)
                        if there(b, p, -1, first, last):
                            turn(*pair(b, p, 1))
                        if there(b, p, 1, first, last):
                            turn_p(*earlier(b, p, 1), 0)
                            turn_p(*earlier(b, p, 1), 1)
                        if p == 1 and not first:
                            project(b - 1)
                        if p == LN_TURN and not last:
                            turn_x(b + 1, PAIRS * b + p + AHEAD)
                        if p + AHEAD < PAIRS:
                            qkv(b, p + AHEAD, xcur, xwhole, None if last else b + 2)
                        elif not last:
                            if p + AHEAD == PAIRS:
                                pe.wait_ge(xx, b + 1)
                            qkv(b + 1, p + AHEAD - PAIRS, xnext, xnew)
                        if p == 1 and not first:
                            pe.wait_ge(res, b)
                        if there(b, p, 1, first, last):
                            values(*earlier(b, p, 1))
                        if p == PAIRS - 1 and not last:
                            pe.wait_ge(xc, b + 2)

                pe.wait_ge(loaded, 16 * LOADS)
                for t in range(TPB):
                    mm = nc.tensor.matmul(ps[:, QB, t * QKW:(t + 1) * QKW], four_sb[:, t * P:(t + 1) * P],
                                          wf_sb[:, :], start=True, stop=True)
                mm.then_inc(fe, 1)
                turn_x(0, 0)
                pe.wait_ge(fs, 1)
                pe.wait_ge(xx, 1)
                qkv(0, 0, xnext, xnew)
                qkv(0, 1, xnext, xnew)
                turn(0, 0)
                qkv(0, 2, xnext, xnew)
                pe.wait_ge(xc, 1)
                batch(0, True, False)
                with pe.Fori(1, BATCH - 1) as b:
                    batch(b, False, False)
                batch(BATCH - 1, False, True)
                for h in range(2):
                    turn_p(BATCH - 1, PAIRS - 1, h)
                values(BATCH - 1, PAIRS - 1)
                project(BATCH - 1)

            @block.vector
            def _(v):
                def rotate(b, p):
                    u = PAIRS * b + p
                    v.wait_ge(qk, u + 1)
                    after(v, tq, u - 1)
                    nc.vector.tensor_tensor(m1[:, p % 2, :], ps[:, QB, :], cos[:, :, :].rearrange("p t c -> p (t c)"),
                                            ALU.mult)
                    q = ps[:, QB, :].rearrange("p (h i s) -> p h s i", h=4 * TPB, s=2)
                    nc.vector.tensor_tensor(
                        m2[:, p % 2, :].rearrange("p (h s i) -> p h s i", h=4 * TPB, s=2), q[:, :, ::-1, :],
                        sin[:, :, :].rearrange("p t (h s i) -> p (t h) s i", h=4, s=2), ALU.mult).then_inc(rope, 1)

                def maximum(b, p, h):
                    u = PAIRS * b + p
                    v.wait_ge(sc, 2 * u + h + 1)
                    nc.vector.tensor_reduce(nmax[:, p % 2, h, :], ps[:, SB + h, :].rearrange("p (t k) -> p t k", t=TPB),
                                            AX.X, ALU.max, negate=True).then_inc(mx, 1)

                def normalise(b, p, h):
                    u = PAIRS * b + p
                    v.wait_ge(ex, 2 * u + h + 1)
                    nc.vector.reciprocal(rinv[:, p % 2, h, :], rsum[:, p % 2, h, :]).then_inc(rc, 1)
                    v.wait_ge(rc, 2 * u + h + 1)
                    for t in range(TPB):
                        mm = nc.vector.tensor_scalar(prob[:, p % 2, h, t, :], prob[:, p % 2, h, t, :],
                                                     rinv[:, p % 2, h, t:t + 1], None, ALU.mult)
                    mm.then_inc(pn, 1)

                def choice(b, k):
                    if k == 0:
                        v.wait_ge(y_in, 16 * (b + 1))
                    after(v, summed, TOPK * b + k)
                    for j in range(TPB):
                        t = bass.ds(TPB * b + j, 1)
                        mm = nc.vector.scalar_tensor_tensor(
                            x[:, t, :], yt[:, t, k * DIM:(k + 1) * DIM],
                            wk[:, t, k:k + 1].rearrange("p a b -> p (a b)"), x[:, t, :], ALU.mult, ALU.add)
                    mm.then_inc(summed, 1)

                def stats(b):
                    v.wait_ge(summed, TOPK * (b + 1))
                    for j in range(TPB):
                        mm = nc.vector.bn_stats(bst[:, j, :], x[:, bass.ds(TPB * b + j, 1), :].rearrange(
                            "p a d -> p (a d)"))
                    mm.then_inc(bn, 1)

                def mean(b):
                    v.wait_ge(bn, b + 1)
                    v.sem_inc(passed_v, 1)
                    for j in range(TPB):
                        mm = nc.vector.bn_aggr(mv[:, j, :], bst[:, j, :])
                    mm.then_inc(agg, 1)
                    v.wait_ge(agg, b + 1)
                    nc.vector.tensor_scalar(st[:, 0, :], mv[:, :, 1], EPS_LN, None, ALU.add).then_inc(var, 1)

                def apply(b):
                    v.wait_ge(rstd, b + 1)
                    after(v, xt, b)
                    for j in range(TPB):
                        mm = nc.vector.tensor_scalar(
                            xn[:, j, :], x[:, bass.ds(TPB * b + j, 1), :].rearrange("p a d -> p (a d)"),
                            mv[:, j, 0:1], st[:, 1, j:j + 1], ALU.subtract, ALU.mult)
                    mm.then_inc(xnd, 1)

                def split(b):
                    v.wait_ge(xev, b + 1)
                    after(v, vp, PAIRS * (b - 1) + AHEAD)
                    after(v, xc, b)
                    nc.vector.tensor_scalar(xtop[:, :].bitcast(I32), xnew[:, :].bitcast(I32), HIGH_BITS, None,
                                            ALU.bitwise_and).then_inc(xh, 1)
                    v.wait_ge(xh, b + 1)
                    nc.vector.tensor_copy(xnext[:, 0, :], xtop[:, :])
                    nc.vector.tensor_tensor(xnext[:, 1, :], xnew[:, :], xtop[:, :], ALU.subtract).then_inc(xx, 1)

                def bias(b):
                    v.wait_ge(xnd, b + 1)
                    xs = x[:, bass.ds(TPB * b, TPB), :]
                    nc.vector.tensor_tensor(xs, xs, bo_sb[:, :].unsqueeze(1).to_broadcast([P, TPB, DIM]),
                                            ALU.add).then_inc(biased, 1)

                def residual(b):
                    v.wait_ge(biased, b + 1)
                    v.wait_ge(op, b + 1)
                    xs = x[:, bass.ds(TPB * b, TPB), :]
                    nc.vector.tensor_tensor(xs, ps[:, OB, 0:SEQ].rearrange("p (t d) -> p t d", t=TPB), xs,
                                            ALU.add).then_inc(res, 1)

                def new_stats(b):
                    v.wait_ge(res, b + 1)
                    for j in range(TPB):
                        mm = nc.vector.bn_stats(bst[:, j, :], x[:, TPB * b + j, :])
                    mm.then_inc(bn, 1)
                    v.wait_ge(bn, BATCH + b + 1)
                    for j in range(TPB):
                        mm = nc.vector.bn_aggr(mv_out[:, TPB * b + j, :], bst[:, j, :])
                    mm.then_inc(agg, 1)
                    v.wait_ge(agg, BATCH + b + 1)

                def batch(b, first, last, more):
                    for p in range(PAIRS):
                        maximum(b, p, 0)
                        if there(b, p, -2, first, last):
                            rotate(*pair(b, p, 2))
                        maximum(b, p, 1)
                        if more:
                            choice(b + 2, p)
                        if not last:
                            if p == LN_STATS:
                                stats(b + 1)
                            if p == LN_MEAN:
                                mean(b + 1)
                            if p == LN_APPLY:
                                apply(b + 1)
                            if p == LN_BIAS:
                                bias(b + 1)
                            if p == LN_TURN:
                                split(b + 1)
                        elif p >= 2:
                            new_stats(p - 2)
                            if p == PAIRS - 1:
                                new_stats(p - 1)
                        normalise(b, p, 0)
                        normalise(b, p, 1)
                        if p == 1 and not first:
                            residual(b - 1)

                for k in range(TOPK):
                    choice(0, k)
                stats(0)
                mean(0)
                apply(0)
                for k in range(TOPK // 2):
                    choice(1, k)
                split(0)
                v.wait_ge(loaded, 16 * LOADS)
                bias(0)
                v.wait_ge(fe, 1)
                nc.vector.tensor_tensor(fenc[:, :, :], ps[:, QB, :].rearrange("p (t c) -> p t c", t=TPB),
                                        bf_sb[:, :].unsqueeze(1).to_broadcast([P, TPB, QKW]), ALU.add
                                        ).then_inc(fs, 1)
                v.wait_ge(fs, 1)
                nc.vector.tensor_scalar(fenc[:, :, 0:P], fenc[:, :, 0:P], SCALE, None, ALU.mult).then_inc(fs, 1)
                rotate(0, 0)
                for k in range(TOPK // 2, TOPK):
                    choice(1, k)
                rotate(0, 1)
                batch(0, True, False, True)
                with v.Fori(1, BATCH - 2) as b:
                    batch(b, False, False, True)
                batch(BATCH - 2, False, False, False)
                batch(BATCH - 1, False, True, False)
                residual(BATCH - 1)

            @block.scalar
            def _(act):
                def take_v(b, p):
                    u = PAIRS * b + p
                    act.wait_ge(vp, u + 1)
                    after(act, pv, 2 * (u - PAIRS + 1))
                    nc.scalar.copy(vsb[:, p, :, :].rearrange("p t d -> p (t d)"), ps[:, VB, 0:TPB * P]
                                   ).then_inc(vev, 1)

                def take_x(b):
                    act.wait_ge(xt, b + 1)
                    after(act, xx, b)
                    after(act, xc, b)
                    after(act, vp, PAIRS * (b - 1) + AHEAD)
                    nc.scalar.copy(xnew[:, :], ps[:, VB, SEQ:]).then_inc(xev, 1)

                def take_qk(b, p):
                    u = PAIRS * b + p
                    act.wait_ge(tq, u + 1)
                    after(act, sc, 2 * (u - 1))
                    nc.scalar.copy(qT[:, p % 2, :], ps[:, TB, 0:SEQ])
                    for h in range(2):
                        r = slice(h * DH, (h + 1) * DH)
                        mm = nc.scalar.copy(kT[r, p % 2, h, :], ps[r, TB, SEQ:])
                    mm.then_inc(qkev, 1)

                def exps(b, p, h):
                    u = PAIRS * b + p
                    act.wait_ge(mx, 2 * u + h + 1)
                    after(act, pt, 2 * (u - 2) + h + 1)
                    for t in range(TPB):
                        mm = nc.scalar.activation(prob[:, p % 2, h, t, :], ps[:, SB + h, t * SEQ:(t + 1) * SEQ],
                                                  ACT.Exp, bias=nmax[:, p % 2, h, t:t + 1],
                                                  accum_out=rsum[:, p % 2, h, t:t + 1])
                    mm.then_inc(ex, 1)

                def take_p(b, p, h):
                    u = PAIRS * b + p
                    act.wait_ge(pt, 2 * u + h + 1)
                    after(act, pv, 2 * (u - 1) + h + 1)
                    nc.scalar.copy(pT[:, h, :, :].rearrange("p j q -> p (j q)"), ps[:, PB + h, :]).then_inc(pte, 1)

                def take_o(b, p):
                    u = PAIRS * b + p
                    act.wait_ge(pv, 2 * u + 2)
                    if p == 0:
                        after(act, op, b)
                    nc.scalar.copy(oT[:, p, :], ps[:, OB, 0:SEQ]).then_inc(oev, 1)

                def batch(b, first, last):
                    for p in range(PAIRS):
                        if there(b, p, 2, first, last):
                            take_o(*earlier(b, p, 2))
                        exps(b, p, 0)
                        if there(b, p, -1, first, last):
                            take_qk(*pair(b, p, 1))
                        if p == LN_TURN and not last:
                            take_x(b + 1)
                        if there(b, p, 1, first, last):
                            take_p(*earlier(b, p, 1), 0)
                            take_p(*earlier(b, p, 1), 1)
                        exps(b, p, 1)
                        if there(b, p, -AHEAD, first, last):
                            take_v(*pair(b, p, AHEAD))

                for dst, src in ((wv_sb[:, :, :], wv), (wo_sb[:, :, :], wout), (wf_sb[:, :], wf),
                                 (four_sb[:, :], four), (bf_sb[:, :], bf), (bo_sb[:, :], bo),
                                 (cos[:, :, :], tabs[0]), (sin[:, :, :], tabs[1])):
                    act.dma_start(dst, src).then_inc(loaded, 16)
                take_x(0)
                act.wait_ge(z, 1)
                take_v(0, 0)
                take_v(0, 1)
                take_qk(0, 0)
                take_v(0, 2)
                batch(0, True, False)
                with act.Fori(1, BATCH - 1) as b:
                    batch(b, False, False)
                batch(BATCH - 1, False, True)
                take_o(BATCH - 1, PAIRS - 2)
                for h in range(2):
                    take_p(BATCH - 1, PAIRS - 1, h)
                take_o(BATCH - 1, PAIRS - 1)


def build(nc, t, out):
    with ExitStack() as ctx:
        def sb(name, shape, dt=F32):
            return ctx.enter_context(nc.sbuf_tensor(name, shape, dt))

        ps = ctx.enter_context(nc.psum_tensor("ps", [P, 8, BLK], F32))
        x = sb("x", [P, TILES, DIM])
        ident = sb("ident", [P, P])
        iota_e = sb("iota_e", [P, EXPERTS], F16)
        iota_p = sb("iota_p", [P, P, TOPK], F16)
        iota_c = sb("iota_c", [P, COLS, TOPK], F16)
        before = sb("before", [P, P], BF16)
        ones_bf = sb("ones_bf", [P, P], BF16)
        tokp1 = sb("tokp1", [P, TILES])
        zeros = sb("zeros", [P, TOPK * DIM])
        xn_dram = nc.dram_tensor("xn_rows", [TOKENS, DIM], F32, kind="Internal").ap()
        y_dram = nc.dram_tensor("y_rows", [YROWS, DIM], F32, kind="Internal").ap()
        x_in = ctx.enter_context(nc.semaphore("x_in"))
        c0 = ctx.enter_context(nc.semaphore("c0"))
        with nc.Block() as block:
            @block.sync
            def _(sp):
                sp.dma_start(x[:, :, :], t["x"].rearrange("(t p) d -> p t d", p=P)).then_inc(x_in, 16)
                sp.wait_ge(x_in, 16)

            @block.vector
            def _(v):
                nc.vector.memset(zeros[:, :], 0.0)
                nc.vector.memset(ones_bf[:, :], 1.0)

            @block.gpsimd
            def _(pool):
                nc.gpsimd.memset(ident[:, :], 1.0).then_inc(c0, 1)
                nc.gpsimd.memset(before[:, :], 1.0).then_inc(c0, 1)
                nc.gpsimd.iota(iota_e[:, :], [[1, EXPERTS]], base=0, channel_multiplier=0,
                               allow_small_or_imprecise_dtypes=True)
                nc.gpsimd.iota(iota_p[:, :, :], [[1, P], [0, TOPK]], base=0, channel_multiplier=0,
                               allow_small_or_imprecise_dtypes=True)
                nc.gpsimd.iota(iota_c[:, :, :], [[1, COLS], [0, TOPK]], base=0, channel_multiplier=0,
                               allow_small_or_imprecise_dtypes=True)
                nc.gpsimd.iota(tokp1[:, :], [[P, TILES]], base=1, channel_multiplier=1,
                               allow_small_or_imprecise_dtypes=True)
                pool.wait_ge(c0, 2)
                nc.gpsimd.affine_select(out=ident[:, :], in_=ident[:, :], compare_op=ALU.is_equal, fill=0.0, base=0,
                                        pattern=[[-1, P]], channel_multiplier=1)
                nc.gpsimd.affine_select(out=before[:, :], in_=before[:, :], compare_op=ALU.is_gt, fill=0.0, base=0,
                                        pattern=[[1, P]], channel_multiplier=-1)

        consts = (ident, iota_e, iota_p, iota_c, before, ones_bf, tokp1, zeros)
        fw = (t["wexp"], t["shw"], t["wg"])
        wk = sb("wk", [P, TILES, TOPK])
        wqh = sb("wqk_high", [P, PAIRS * 2 * P], F32R)
        wql = sb("wqk_low", [P, PAIRS * 2 * P], F32R)
        mv = sb("mv", [P, TILES, 2])
        experts(nc, x, wk, consts, fw, y_dram, xn_dram, ps, "f1", True, mv, 0, (t["wqk"], wqh, wql))
        qk_parts = [w.rearrange("p (a c) -> p a c", a=PAIRS) for w in (wqh[:, :], wql[:, :])]
        attn_w = (qk_parts, t["wv"], t["wout"], t["wf"], t["bf"], t["bo"], (t["cos"], t["sin"]), t["four"])
        attention(nc, x, wk, y_dram, attn_w, consts, ps, mv)
        experts(nc, x, wk, consts, fw, y_dram, xn_dram, ps, "f2", False, mv, TILES - TPB)
        weighted_sum(nc, x, wk, ident, y_dram, out, ps)


def tables():
    pos = np.arange(SEQ, dtype=np.float32)[:, None]
    freqs = np.float32(10000.0) ** (-np.arange(0, DH, 2, dtype=np.float32) / np.float32(DH))
    ang = np.repeat(pos * freqs.astype(np.float32), 2, axis=1)
    sin, cos = np.sin(ang), np.cos(ang)
    sign = np.where(np.arange(DH) < DH // 2, -1.0, 1.0).astype(np.float32)
    pf = pos * np.arange(1, FREQS + 1, dtype=np.float32)
    four = np.concatenate([np.sin(pf), np.cos(pf)], axis=1).T

    def tile(a):
        a = a.reshape(TPB, P, DH).transpose(1, 0, 2).astype(np.float32)
        return np.concatenate([np.float32(SCALE) * a] * 2 + [a] * 2, axis=2)
    return tile(cos), tile(sin * sign), np.ascontiguousarray(four).astype(np.float32)


def kernel(L0_attn_x, L0_attn_w_qkv, L0_attn_w_fproj, L0_attn_b_fproj, L0_attn_w_out, L0_attn_b_out, L0_ffn_wg,
           L0_ffn_shared_w1, L0_ffn_shared_w2, L0_ffn_expert_w1, L0_ffn_expert_w2):
    import concourse.bacc as bacc
    from concourse.bass_utils import run_bass_kernel_spmd

    def joined(w1, w2):
        a = np.asarray(w1).transpose(0, 2, 1)
        b = np.asarray(w2).transpose(0, 2, 1).reshape(-1, FC, P, DIM).transpose(0, 2, 1, 3).reshape(-1, P, FC * DIM)
        return np.ascontiguousarray(np.concatenate([a, b], axis=2))

    wqkv = np.asarray(L0_attn_w_qkv).reshape(3, PAIRS, P, DIM).transpose(3, 1, 0, 2)
    wout = np.asarray(L0_attn_w_out).T.reshape(PAIRS, P, DIM).transpose(1, 0, 2)
    wf = np.asarray(L0_attn_w_fproj).T
    bf = np.asarray(L0_attn_b_fproj)
    cos, sin, four = tables()
    arrays = {
        "x": np.asarray(L0_attn_x).reshape(TOKENS, DIM),
        "wexp": joined(L0_ffn_expert_w1, L0_ffn_expert_w2),
        "shw": joined(np.asarray(L0_ffn_shared_w1)[None], np.asarray(L0_ffn_shared_w2)[None])[0],
        "wg": np.concatenate([np.asarray(L0_ffn_wg).T] * 2, axis=1),
        "wqk": wqkv[:, :, 0:2].reshape(DIM, PAIRS * 2 * P), "wv": wqkv[:, :, 2], "wout": wout,
        "wf": np.concatenate([wf] * 4, axis=1), "bf": np.broadcast_to(np.concatenate([bf] * 4), (P, 4 * DH)),
        "bo": np.broadcast_to(np.asarray(L0_attn_b_out), (P, DIM)),
        "cos": cos, "sin": sin, "four": four,
    }
    arrays = {n: np.ascontiguousarray(a) for n, a in arrays.items()}
    nc = bacc.Bacc("TRN2", target_bir_lowering=False, num_devices=1)
    t = {n: nc.dram_tensor(f"in_{n}", a.shape, mybir.dt.from_np(a.dtype), kind="ExternalInput").ap()
         for n, a in arrays.items()}
    out = nc.dram_tensor("out", [TOKENS, DIM], F32, kind="ExternalOutput").ap()
    build(nc, t, out)
    r = run_bass_kernel_spmd(nc, [{f"in_{n}": a for n, a in arrays.items()}], core_ids=[0])
    return r.results[0]["out"].reshape(BATCH, SEQ, DIM)
```
